# Optimizing a Trainium2 kernel written in Bass

```python
import numpy as np
import jax
import jax.numpy as jnp

def _softmax(x, axis=-1):
    return jax.nn.softmax(x, axis=axis)

def _gelu(x):
    return jax.nn.gelu(x, approximate=True)

def _silu(x):
    return jax.nn.silu(x)

def _sigmoid(x):
    return jax.nn.sigmoid(x)

def _layernorm(x, axis=-1, eps=1e-05):
    m = jnp.mean(x, axis=axis, keepdims=True)
    v = jnp.var(x, axis=axis, keepdims=True)
    return (x - m) / jnp.sqrt(v + eps)

def _scatter_add(tgt, idx, src, axis=0):
    return tgt.at[idx].add(src)

def _segment_sum(src, seg, n):
    return jax.ops.segment_sum(src, seg, n)
kernel_name = 'mk_adaln_d1_jaxref_r4_e0b12a'

def setup_inputs(seed: int=0):
    np.random.seed(seed)
    _w = jnp.asarray

    def _L0_attn_setup():
        import jax, jax.numpy as jnp
        import numpy as np
        key = jax.random.key(seed)
        k1, k2, k3 = jax.random.split(key, 3)
        N, S, D = (8, 512, 256)
        x = jax.random.normal(k1, (N, S, D), dtype=jnp.float32)
        std = np.sqrt(2.0 / D).astype(np.float32)
        w_lhs = jax.random.normal(k2, (1, 1, D), dtype=jnp.float32) * std
        w_rhs = jax.random.normal(k3, (1, 1, D), dtype=jnp.float32) * std
        return {'x': x, 'w_lhs': w_lhs, 'w_rhs': w_rhs}
    _L0_attn_in = _L0_attn_setup()

    def _L0_ffn_setup():
        import jax, jax.numpy as jnp
        import numpy as np
        HIDDEN = 256
        INTER = 1024
        key = jax.random.key(seed)
        k1, k2, k3, k4, k5 = jax.random.split(key, 5)
        hidden_states = jax.random.normal(k1, (4, 512, HIDDEN), dtype=jnp.float32)
        W1 = jax.random.normal(k2, (HIDDEN, INTER), dtype=jnp.float32) * (1.0 / np.sqrt(HIDDEN))
        b1 = jax.random.normal(k3, (INTER,), dtype=jnp.float32) * 0.02
        W2 = jax.random.normal(k4, (INTER, HIDDEN), dtype=jnp.float32) * (1.0 / np.sqrt(INTER))
        b2 = jax.random.normal(k5, (HIDDEN,), dtype=jnp.float32) * 0.02
        return {'hidden_states': hidden_states, 'W1': W1, 'b1': b1, 'W2': W2, 'b2': b2}
    _L0_ffn_in = _L0_ffn_setup()
    _L0_c = _w((lambda *s: np.random.randn(*s).astype(np.float32) * 0.05)(8, 256))
    _L0_wmod = _w((lambda *s: np.random.randn(*s).astype(np.float32) * 0.05)(256, 6 * 256) * 256 ** (-0.5))
    _d = {'L0_attn_x': _L0_attn_in['x'], 'L0_attn_w_lhs': _L0_attn_in['w_lhs'], 'L0_attn_w_rhs': _L0_attn_in['w_rhs'], 'L0_ffn_W1': _L0_ffn_in['W1'], 'L0_ffn_b1': _L0_ffn_in['b1'], 'L0_ffn_W2': _L0_ffn_in['W2'], 'L0_ffn_b2': _L0_ffn_in['b2'], 'L0_c': _L0_c, 'L0_wmod': _L0_wmod}
    _x0 = _d['L0_attn_x']
    _d['L0_attn_x'] = jax.random.normal(jax.random.fold_in(jax.random.key(seed), 1), (8, 1024, 256), dtype=_x0.dtype)
    del _x0
    return _d

def reference(L0_attn_x, L0_attn_w_lhs, L0_attn_w_rhs, L0_ffn_W1, L0_ffn_b1, L0_ffn_W2, L0_ffn_b2, L0_c, L0_wmod):

    def _L0_attn_ref(x, w_lhs, w_rhs):
        import jax, jax.numpy as jnp
        import numpy as np
        lhs = x * w_lhs
        rhs = x * w_rhs
        scores = jnp.einsum('nsd,ntd->nst', lhs, rhs)
        attn = jax.nn.softmax(scores, axis=2)
        return jnp.einsum('nst,ntd->nsd', attn, x)

    def _L0_ffn_ref(hidden_states, W1, b1, W2, b2):
        import jax, jax.numpy as jnp
        import numpy as np
        HIDDEN = 256
        INTER = 1024
        h = jax.nn.relu(jnp.einsum('bsh,hi->bsi', hidden_states, W1) + b1)
        return jnp.einsum('bsi,ih->bsh', h, W2) + b2
    x = L0_attn_x
    mod = (_silu(L0_c) @ L0_wmod).reshape(L0_c.shape[0], 6, 1, -1)
    sa, ca, ga, sb, cb, gb = (mod[:, 0], mod[:, 1], mod[:, 2], mod[:, 3], mod[:, 4], mod[:, 5])
    ga = (2 * (ga >= 0) - 1) * jnp.maximum(jnp.abs(ga), 0.25)
    gb = (2 * (gb >= 0) - 1) * jnp.maximum(jnp.abs(gb), 0.25)
    h = _layernorm(x, axis=-1) * (1 + ca) + sa
    x = x + ga * _L0_attn_ref(h, L0_attn_w_lhs, L0_attn_w_rhs)
    h = _layernorm(x, axis=-1) * (1 + cb) + sb
    x = x + gb * _L0_ffn_ref(h, L0_ffn_W1, L0_ffn_b1, L0_ffn_W2, L0_ffn_b2)
    return x

_drawn_inputs = setup_inputs


def setup_inputs(seed=0):
    import zlib

    import numpy as np

    out = dict(_drawn_inputs(seed))
    spreads = {}
    factors = {'L0_attn_w_lhs': 8.0, 'L0_attn_w_rhs': 8.0, 'L0_ffn_b1': 8.0, 'L0_ffn_b2': 8.0}
    for name, (base, spread) in spreads.items():
        noise = np.random.default_rng([zlib.crc32(name.encode()), seed]).standard_normal(out[name].shape)
        drawn = base * np.exp(spread * noise) if base else spread * noise
        out[name] = jnp.asarray(drawn.astype(out[name].dtype))
    for name, factor in factors.items():
        out[name] = (out[name] * factor).astype(out[name].dtype)
    return out
```

```python
from contextlib import ExitStack

import concourse.bass as bass
from concourse import mybir

F32 = mybir.dt.float32
F32R = mybir.dt.float32r
ALU = mybir.AluOpType
ACT = mybir.ActivationFunctionType

P = 128
EPS = 1e-5

STEPS = [
    ("L2", 1, "prev"), ("SC", 0, "this"), ("SC", 1, "this"), ("F", 0, "prev"), ("XG", 2, "prev"),
    ("SC", 2, "this"), ("XG", 3, "prev"), ("T2", 1, "prev"), ("VL", 0, "this"), ("SC", 3, "this"),
    ("F", 1, "prev"), ("XC", 0, "this"), ("SC", 4, "this"), ("V", 0, "this"), ("F", 2, "prev"),
    ("XC", 1, "this"), ("SC", 5, "this"), ("F", 3, "prev"), ("VL", 1, "this"), ("SC", 6, "this"),
    ("F", 4, "prev"), ("SC", 7, "this"), ("F", 5, "prev"), ("MT", 0, "this"), ("V", 1, "this"),
    ("XC", 2, "this"), ("F", 6, "prev"),
    ("MB", 0, "this"), ("SM", 0, "this"), ("L1", 0, "next"), ("F", 7, "prev"), ("SM", 1, "this"),
    ("XC", 3, "this"), ("F", 8, "prev"), ("SM", 2, "this"), ("AV", 0, "this"), ("F", 9, "prev"),
    ("OUT", 0, "prev"), ("TH", 0, "next"), ("SM", 3, "this"), ("AV", 1, "this"), ("F", 10, "prev"),
    ("L1", 1, "next"), ("SM", 4, "this"), ("AV", 2, "this"), ("F", 11, "prev"), ("SM", 5, "this"),
    ("AV", 3, "this"), ("F", 12, "prev"), ("TH", 1, "next"), ("SM", 6, "this"), ("AV", 4, "this"),
    ("L2", 0, "this"), ("F", 13, "prev"), ("SM", 7, "this"), ("AV", 5, "this"), ("T2", 0, "this"),
    ("XG", 0, "this"), ("F", 14, "prev"), ("AV", 6, "this"), ("XG", 1, "this"), ("F", 15, "prev"),
    ("AV", 7, "this"), ("DR", 0, "prev"), ("OUT", 1, "prev"),
]


class Phase:

    def __init__(self, batches, which, col_base, feature_base):
        self.steps = [(kind, n) for kind, n, which_batch in STEPS if which_batch in which]
        self.has = which
        self.col_base = col_base
        self.feature_base = feature_base

    def jobs(self, weights, until=None):
        total = 0
        for step in self.steps:
            if step == until:
                break
            total += weights.get(step[0], 0)
        return total


COL_JOBS = {"F": 1, "T2": 2, "TH": 2}
FEATURE_JOBS = {"T2": 2, "TH": 2}


def phases(NB):
    made = {}

    def add(name, which, col_base, feature_base):
        made[name] = Phase(NB, which, col_base, feature_base)
        return made[name].jobs(COL_JOBS), made[name].jobs(FEATURE_JOBS)

    c0, f0 = add("before", {"next"}, lambda b: 0, lambda b: 0)
    c1, f1 = add("first", {"this", "next"}, lambda b: c0, lambda b: f0)
    c1, f1 = c0 + c1, f0 + f1
    cm, fm = add("middle", {"prev", "this", "next"}, lambda b: b * cm + (c1 - cm), lambda b: b * fm + (f1 - fm))
    cl, fl = add("last", {"prev", "this"}, lambda b: c1 + (NB - 2) * cm, lambda b: f1 + (NB - 2) * fm)
    add("after", {"prev"}, lambda b: c1 + (NB - 2) * cm + cl, lambda b: f1 + (NB - 2) * fm + fl)
    return made


def block_kernel(nc, x, w_lhs, w_rhs, W1, b1, W2, b2, cT, wmod, out):
    NB, ROWS, D = x.shape
    FF = W1.shape[1]
    T = ROWS // P
    DK = D // P
    FT = FF // P
    HR = ROWS // 2
    HT = T // 2
    RING = 3
    VW = D + 2
    assert T == 8 and DK == 2 and FT == 8 and HR == 512 and NB >= 3
    NF = 2 * FT

    first_col = [P * j for j in range(T)]
    first_col[3], first_col[7] = 2 * P, 6 * P

    PH = phases(NB)
    rows = lambda b, h, dram: dram[b, h * HR:(h + 1) * HR, :].rearrange("(t p) d -> p t d", p=P)
    x_rows = x.rearrange("b (h t p) d -> b h p t d", p=P, h=2)
    out_rows = out.rearrange("b (h t p) d -> b h p t d", p=P, h=2)
    mod_rows = nc.dram_tensor("mod_rows", [NB, 4, D], F32, kind="Internal").ap()

    with ExitStack() as ctx:
        sb = lambda name, shape, dt=F32: ctx.enter_context(nc.sbuf_tensor(name, shape, dt))
        psum = lambda name, shape: ctx.enter_context(nc.psum_tensor(name, shape, F32))
        sem = lambda name: ctx.enter_context(nc.semaphore(name))

        ident = sb("ident", [P, P])
        select = sb("select", [2 * T, T, P], F32R)
        W1hi, W1lo = sb("W1hi", [P, DK, FF], F32R), sb("W1lo", [P, DK, FF], F32R)
        W2hi, W2lo = sb("W2hi", [P, FT, D], F32R), sb("W2lo", [P, FT, D], F32R)
        b1T = sb("b1T", [P, FT])
        wl, wr = sb("wl", [P, DK]), sb("wr", [P, DK])
        mod_cols = sb("mod_cols", [P, NB, 4 * DK])
        mod_a, mod_b = sb("mod_a", [P, 2 * DK]), sb("mod_b", [P, 2 * DK])
        attn_mod, gb_b2, gb_all = sb("attn_mod", [P, 2, D]), sb("gb_b2", [P, D]), sb("gb_all", [P, D])
        S = sb("S", [P, T, ROWS])
        Phi, Plo = sb("Phi", [P, RING, T, P], F32R), sb("Plo", [P, RING, T, P], F32R)
        Lhi, Llo = sb("Lhi", [P, DK, ROWS], F32R), sb("Llo", [P, DK, ROWS], F32R)
        Rhi, Rlo = sb("Rhi", [P, DK, ROWS], F32R), sb("Rlo", [P, DK, ROWS], F32R)
        V = sb("V", [P, T, 2 * VW], F32R)
        x_cur = sb("x_cur", [P, T, D])
        x_mlp = sb("x_mlp", [P, T, D])
        ln1, ln2 = sb("ln1", [P, HT, D]), sb("ln2", [P, HT, D])
        featT = sb("featT", [P, DK, HR])
        hid = sb("hid", [P, 2, HR])
        hid_hi, hid_lo = sb("hid_hi", [P, RING, HR], F32R), sb("hid_lo", [P, RING, HR], F32R)
        h2hi, h2lo = sb("h2hi", [P, DK, ROWS], F32R), sb("h2lo", [P, DK, ROWS], F32R)
        stats, stats1 = sb("stats", [P, HT, 6]), sb("stats1", [P, HT, 6])
        mv1, nm1, rs1 = sb("mv1", [P, T, 2]), sb("nm1", [P, T]), sb("rs1", [P, T])
        mv2, nm2, rs2 = sb("mv2", [P, T, 2]), sb("nm2", [P, T]), sb("rs2", [P, T])
        var_eps, half_power = sb("var_eps", [P, HT]), sb("half_power", [P, HT])
        row_max, neg_max = sb("row_max", [P, T]), sb("neg_max", [P, 2 * T], F32R)
        neg_maxT = Phi[0:2 * T, RING - 1, 0, :]
        inv_sum = sb("inv_sum", [P, 1])

        wmod_sb = S[:, 0:3, :].rearrange("p a b -> p (a b)").rearrange("p (k n) -> p k n", k=DK)
        W1_sb = S[:, 3:5, :]
        W2_sb = S[:, 5:7, :].rearrange("p a (i d) -> p (a i) d", d=D)
        select_sb = S[0:2 * T, 7, :].rearrange("p (j c) -> p j c", c=P)
        cT_sb = hid[:, 0, 0:DK * NB].rearrange("p (k b) -> p k b", b=NB)
        siluT = hid[:, 0, 64:64 + DK * NB].rearrange("p (k b) -> p k b", b=NB)
        sig = hid[:, 1, 0:DK * NB].rearrange("p (k b) -> p k b", b=NB)
        sig1 = hid[:, 1, 64:64 + DK * NB].rearrange("p (k b) -> p k b", b=NB)
        sig2 = hid[:, 1, 128:128 + DK * NB].rearrange("p (k b) -> p k b", b=NB)
        b2_sb = x_mlp[0:NB, 7, :]
        mods = x_mlp[0:NB, 0:4, :]
        signs, mags = ln2[0:NB, 0:2, :], ln2[0:NB, 2:4, :]
        mod_out = x_mlp[0:NB, 4:7, :]
        gb_out = ln2[0:NB, 3, :]

        score = [psum("score0", [P, ROWS]), psum("score1", [P, ROWS])]
        col = [psum("col0", [P, HR]), psum("col1", [P, HR])]
        acc = psum("acc", [P, 2, 2, D])
        maxT_ps = score[0][0:2 * T, 0:P]
        max_ps = score[1]
        av_ps = [score[0][:, 0:VW], score[0][:, HR:HR + VW]]

        small_in, wmod_in, w_in, b2_in = sem("small_in"), sem("wmod_in"), sem("w_in"), sem("b2_in")
        mods_stored = sem("mods_stored")
        ln1_in = sem("ln1_in")
        x_in = [sem("x_in0"), sem("x_in1")]
        attn_mod_in, gb_b2_in, gb_in = sem("attn_mod_in"), sem("gb_b2_in"), sem("gb_in")
        stored = [sem("stored0"), sem("stored1")]
        passed = sem("passed")
        const_ready, pool_const = sem("const_ready"), sem("pool_const")
        silu_step, sig_step = sem("silu_step"), sem("sig_step")
        modT_mm, mod_mm, mod_step = sem("modT_mm"), sem("mod_mm"), sem("mod_step")
        modT_ready, mods_ready = sem("modT_ready"), sem("mods_ready")
        w_hi_ready, w_ready = sem("w_hi_ready"), sem("w_ready")
        scores_done, scores_read = sem("scores_done"), sem("scores_read")
        maxT_step, maxT_done, maxT_ready, max_done = sem("maxT_step"), sem("maxT_done"), sem("maxT_ready"), sem("max_done")
        sub_done, exp_done, phi_done, plo_done = sem("sub_done"), sem("exp_done"), sem("phi_done"), sem("plo_done")
        av_done, av_read, inv_ready = sem("av_done"), sem("av_read"), sem("inv_ready")
        av_scaled, x2_stats, x2_mv = sem("av_scaled"), sem("x2_stats"), sem("x2_mv")
        xc_done, xg_done = sem("xc_done"), sem("xg_done")
        ln1_stats, ln1_mv, ln1_eps, ln1_rstd, ln1_done = sem("ln1_stats"), sem("ln1_mv"), sem("ln1_eps"), sem("ln1_rstd"), sem("ln1_done")
        ln2_eps, ln2_rstd, ln2_done = sem("ln2_eps"), sem("ln2_rstd"), sem("ln2_done")
        v_ln, v_hi, v_done = sem("v_ln"), sem("v_hi"), sem("v_done")
        col_done, col_read = sem("col_done"), sem("col_read")
        mod_a_ready, mod_b_ready = sem("mod_a_ready"), sem("mod_b_ready")
        feat_hi, feat_done = sem("feat_hi"), sem("feat_done")
        hid_hi_done, hid_lo_done = sem("hid_hi_done"), sem("hid_lo_done")
        acc_done, acc_mul, out_done = sem("acc_done"), sem("acc_mul"), sem("out_done")

        def wait(eng, semaphore, value):
            if not (isinstance(value, int) and value <= 0):
                eng.wait_ge(semaphore, value)

        def wait_apart(eng, semaphore, value):
            eng.wait_ge(semaphore, value)
            eng.sem_inc(passed, 1)

        def over_batches(eng, part):
            part(-1, PH["before"])
            part(0, PH["first"])
            with eng.Fori(1, NB - 1) as b:
                part(b, PH["middle"])
            part(NB - 1, PH["last"])
            part(NB, PH["after"])

        block = ctx.enter_context(nc.Block())

        @block.sync
        def _(sp):
            sp.sem_inc(stored[1], 16)
            sp.dma_start(cT_sb, cT.rearrange("(k p) b -> p k b", p=P)).then_inc(small_in, 16)
            sp.dma_start(b1T[:], b1).then_inc(small_in, 16)
            sp.dma_start(wl[:], w_lhs).then_inc(small_in, 16)
            sp.dma_start(wr[:], w_rhs).then_inc(small_in, 16)
            sp.dma_start(ln1[:], x_rows[0, 0]).then_inc(ln1_in, 16)
            sp.dma_start(wmod_sb, wmod.rearrange("(k p) n -> p k n", p=P)).then_inc(wmod_in, 16)
            sp.dma_start(b2_sb, b2.partition_broadcast(NB)).then_inc(b2_in, 16)
            sp.dma_start(W1_sb, W1.rearrange("(k p) n -> p k n", p=P)).then_inc(w_in, 16)
            sp.dma_start(W2_sb, W2.rearrange("(i p) d -> p i d", p=P)).then_inc(w_in, 16)
            sp.dma_start(x_cur[:, 0:HT, :], x_rows[0, 0]).then_inc(x_in[0], 16)
            sp.wait_ge(col_done, DK)
            sp.dma_start(ln1[:], x_rows[0, 1]).then_inc(ln1_in, 16)
            sp.wait_ge(mods_ready, 1)
            sp.dma_start(mod_rows[:, 0:3, :], mod_out).then_inc(mods_stored, 16)
            sp.dma_start(mod_rows[:, 3, :], gb_out).then_inc(mods_stored, 16)
            sp.wait_ge(mods_stored, 32)

            def part(b, ph):
                f = b - 1
                if "this" in ph.has:
                    wait(sp, av_read, T * b)
                    sp.dma_start(attn_mod[:].rearrange("p a d -> p (a d)"),
                                 mod_rows[b, 0:2, :].rearrange("a d -> (a d)").partition_broadcast(P)).then_inc(attn_mod_in, 16)
                if "prev" in ph.has:
                    sp.dma_start(gb_all[:], mod_rows[f, 3, :].partition_broadcast(P)).then_inc(gb_in, 16)
                if "this" in ph.has:
                    wait(sp, xg_done, T // 2 * b)
                    sp.dma_start(x_cur[:, HT:T, :], x_rows[b, 1]).then_inc(x_in[1], 16)
                    sp.dma_start(gb_b2[:], mod_rows[b, 2, :].partition_broadcast(P)).then_inc(gb_b2_in, 16)
                if "next" in ph.has:
                    sp.wait_ge(v_done, 2 * b + 2)
                    sp.dma_start(ln1[:], x_rows[b + 1, 0]).then_inc(ln1_in, 16)
                if "prev" in ph.has:
                    sp.wait_ge(out_done, 4 * f + 2)
                    sp.dma_start(out_rows[f, 0], x_mlp[:, 0:HT, :]).then_inc(stored[0], 16)
                if "next" in ph.has:
                    sp.wait_ge(col_done, ph.col_base(b) + ph.jobs(COL_JOBS, ("TH", 0)) + DK)
                    sp.dma_start(ln1[:], x_rows[b + 1, 1]).then_inc(ln1_in, 16)
                    sp.wait_ge(xg_done, T // 2 * b + 2)
                    sp.dma_start(x_cur[:, 0:HT, :], x_rows[b + 1, 0]).then_inc(x_in[0], 16)
                if "prev" in ph.has:
                    sp.wait_ge(out_done, 4 * f + 4)
                    sp.dma_start(out_rows[f, 1], x_mlp[:, HT:T, :]).then_inc(stored[1], 16)

            part(0, PH["first"])
            with sp.Fori(1, NB - 1) as b:
                part(b, PH["middle"])
            part(NB - 1, PH["last"])
            part(NB, PH["after"])
            for h in range(2):
                sp.wait_ge(stored[h], 16 * (NB + h))

        @block.tensor
        def _(pe):
            pe.wait_ge(silu_step, 1)
            pe.wait_ge(wmod_in, 16)
            for n, m in enumerate((1, 0, 4, 3)):
                for k in range(DK):
                    for kk in range(DK):
                        last = nc.tensor.matmul(acc[:, 0, 0, (n * DK + k) * NB:(n * DK + k + 1) * NB],
                                                wmod_sb[:, kk, m * D + k * P:m * D + (k + 1) * P], siluT[:, kk, :],
                                                start=(kk == 0), stop=(kk == DK - 1))
            last.then_inc(modT_mm, 1)
            for bank, at, m, width in ((0, 0, 0, 2), (1, 0, 2, 1), (1, HR, 5, 1)):
                for kk in range(DK):
                    last = nc.tensor.matmul(score[bank][0:NB, at:at + width * D], siluT[:, kk, :],
                                            wmod_sb[:, kk, m * D:(m + width) * D], start=(kk == 0), stop=(kk == DK - 1))
            last.then_inc(mod_mm, 1)
            pe.wait_ge(pool_const, 2)

            def part(b, ph):
                f = b - 1
                column, features = ph.col_base(b), ph.feature_base(b)

                def second_layer(i):
                    slot, it = i % RING, i % FT
                    pe.wait_ge(hid_lo_done, NF * f + i + 1)
                    if i == 0:
                        pe.wait_ge(xg_done, T // 2 * f + T // 2)
                    elif it == 0:
                        pe.wait_ge(out_done, 4 * f + 2)
                    for t in range(HT):
                        o = acc[:, t // 2, t % 2, :]
                        hi = hid_hi[:, slot, t * P:(t + 1) * P]
                        lo = hid_lo[:, slot, t * P:(t + 1) * P]
                        nc.tensor.matmul(o, hi, W2hi[:, it, :], start=(it == 0 and t % 2 == 0), stop=False, skip_group_check=True)
                        nc.tensor.matmul(o, hi, W2lo[:, it, :], start=False, stop=False, skip_group_check=True)
                        last = nc.tensor.matmul(o, lo, W2hi[:, it, :], start=False, stop=(it == FT - 1), skip_group_check=True)
                    last.then_inc(acc_done, 1)

                for step, (kind, n) in enumerate(ph.steps):
                    c = column + ph.jobs(COL_JOBS, (kind, n))
                    cb = ph.jobs(COL_JOBS, (kind, n)) % 2
                    if kind == "SC":
                        if n == 0:
                            pe.wait_ge(feat_done, features)
                            wait(pe, av_read, T * b)
                            if ph is PH["first"]:
                                pe.wait_ge(mods_ready, 1)
                        elif n == 1:
                            wait(pe, sub_done, T * b)
                        else:
                            pe.wait_ge(scores_read, T * b + n - 1)
                        at = first_col[n]
                        for lo_col in range(0, ROWS, HR):
                            start_col = max(at, lo_col)
                            width = lo_col + HR - start_col
                            if width <= 0:
                                continue
                            o = score[n % 2][:, start_col:lo_col + HR]
                            tile, cols = slice(n * P, (n + 1) * P), slice(start_col, lo_col + HR)
                            for kk in range(DK):
                                nc.tensor.matmul(o, Lhi[:, kk, tile], Rhi[:, kk, cols], start=(kk == 0), stop=False)
                                nc.tensor.matmul(o, Lhi[:, kk, tile], Rlo[:, kk, cols], start=False, stop=False)
                                last = nc.tensor.matmul(o, Llo[:, kk, tile], Rhi[:, kk, cols], start=False, stop=(kk == DK - 1))
                        for i in range(at // P):
                            if i == at // P - 1:
                                pe.wait_ge(scores_read, T * b + i + 1)
                            last = nc.tensor.transpose(score[n % 2][:, i * P:(i + 1) * P], S[:, i, n * P:(n + 1) * P], ident[:])
                        last.then_inc(scores_done, 1)
                    elif kind == "F":
                        half, it = n // FT, n % FT
                        if it == 0:
                            pe.wait_ge(feat_done, features + DK * half)
                        pe.wait_ge(col_read, c - 1)
                        tile, cols = slice(it * P, (it + 1) * P), slice(half * HR, (half + 1) * HR)
                        for kk in range(DK):
                            nc.tensor.matmul(col[cb][:], W1hi[:, kk, tile], h2hi[:, kk, cols], start=(kk == 0), stop=False)
                            nc.tensor.matmul(col[cb][:], W1hi[:, kk, tile], h2lo[:, kk, cols], start=False, stop=False)
                            last = nc.tensor.matmul(col[cb][:], W1lo[:, kk, tile], h2hi[:, kk, cols], start=False, stop=(kk == DK - 1))
                        last.then_inc(col_done, 1)
                        if n >= 2:
                            second_layer(n - 2)
                    elif kind == "DR":
                        second_layer(NF - 2)
                        second_layer(NF - 1)
                    elif kind in ("TH", "T2"):
                        if kind == "TH":
                            pe.wait_ge(ln1_done, 2 * (b + 1) + n + 1)
                            ln = ln1
                        else:
                            pe.wait_ge(ln2_done, 2 * (b if n == 0 else f) + n + 1)
                            ln = ln2
                        for kk in range(DK):
                            wait(pe, col_read, c + kk - 1)
                            for t in range(HT):
                                last = nc.tensor.transpose(col[(cb + kk) % 2][:, t * P:(t + 1) * P], ln[:, t, kk * P:(kk + 1) * P], ident[:])
                            last.then_inc(col_done, 1)
                    elif kind == "MT":
                        if ph is PH["first"]:
                            pe.wait_ge(w_ready, 4)
                        pe.wait_ge(maxT_step, 2 * b + 2)
                        nc.tensor.transpose(maxT_ps, neg_max[:].bitcast(F32), ident[:]).then_inc(maxT_done, 1)
                    elif kind == "MB":
                        pe.wait_ge(maxT_ready, b + 1)
                        for j in range(T):
                            last = nc.tensor.matmul(max_ps[:, j * P:(j + 1) * P], select[:, j, :], neg_maxT, start=True, stop=True)
                        last.then_inc(max_done, 1)
                    elif kind == "AV":
                        pe.wait_ge(plo_done, T * b + n + 1)
                        if n == 0:
                            pe.wait_ge(v_done, 2 * b + 2)
                        if n >= 2:
                            pe.wait_ge(av_read, T * b + n - 1)
                        slot, o = n % RING, av_ps[n % 2]
                        for t in range(T):
                            nc.tensor.matmul(o, Phi[:, slot, t, :], V[:, t, 0:VW], start=(t == 0), stop=False)
                            nc.tensor.matmul(o[:, 0:D], Phi[:, slot, t, :], V[:, t, VW:VW + D], start=False, stop=False)
                            last = nc.tensor.matmul(o, Plo[:, slot, t, :], V[:, t, VW:2 * VW], start=False, stop=(t == T - 1))
                        last.then_inc(av_done, 1)

            over_batches(pe, part)

        @block.scalar
        def _(act):
            act.wait_ge(small_in, 64)
            nc.scalar.activation(sig, cT_sb, ACT.Exp, scale=-1.0).then_inc(sig_step, 1)
            act.wait_ge(w_in, 32)
            nc.scalar.activation(W1hi[:], W1_sb, ACT.Copy).then_inc(w_hi_ready, 1)
            nc.scalar.activation(W2hi[:], W2_sb, ACT.Copy).then_inc(w_hi_ready, 1)
            act.wait_ge(modT_ready, 4)

            def part(b, ph):
                f = b - 1
                column, features = ph.col_base(b), ph.feature_base(b)
                for kind, n in ph.steps:
                    c = column + ph.jobs(COL_JOBS, (kind, n))
                    cb = ph.jobs(COL_JOBS, (kind, n)) % 2
                    q = features + ph.jobs(FEATURE_JOBS, (kind, n))
                    if kind == "F":
                        act.wait_ge(col_done, c + 1)
                        if n >= 2:
                            act.wait_ge(hid_lo_done, NF * f + n - 1)
                        nc.scalar.activation(hid[:, n % 2, :], col[cb][:], ACT.Relu, bias=b1T[:, n % FT:n % FT + 1]).then_inc(col_read, 1)
                        act.wait_ge(col_read, c + 1)
                        if n >= RING:
                            act.wait_ge(acc_done, NF * f + n - RING + 1)
                        nc.scalar.activation(hid_hi[:, n % RING, :], hid[:, n % 2, :], ACT.Copy).then_inc(hid_hi_done, 1)
                    elif kind in ("TH", "T2"):
                        half = n
                        mod = mod_a if kind == "TH" else mod_b
                        if kind == "TH":
                            act.wait_ge(mod_a_ready, b + 2)
                        else:
                            act.wait_ge(mod_b_ready, (b if n == 0 else f) + 1)
                        cols = slice(half * HR, (half + 1) * HR)
                        for kk in range(DK):
                            act.wait_ge(col_done, c + kk + 1)
                            wait(act, feat_done, q + kk - 1)
                            nc.scalar.activation(featT[:, kk, :], col[(cb + kk) % 2][:], ACT.Identity,
                                                 scale=mod[:, kk:kk + 1], bias=mod[:, DK + kk:DK + kk + 1]).then_inc(col_read, 1)
                            act.wait_ge(col_read, c + kk + 1)
                            if kind == "TH":
                                nc.scalar.activation(Lhi[:, kk, cols], featT[:, kk, :], ACT.Copy, scale=wl[:, kk:kk + 1])
                                nc.scalar.activation(Rhi[:, kk, cols], featT[:, kk, :], ACT.Copy, scale=wr[:, kk:kk + 1]).then_inc(feat_hi, 1)
                            else:
                                nc.scalar.activation(h2hi[:, kk, cols], featT[:, kk, :], ACT.Copy).then_inc(feat_hi, 1)
                    elif kind == "L1" and n == 0:
                        nc.scalar.activation(mod_a[:], mod_cols[:, b + 1, 0:2 * DK], ACT.Copy).then_inc(mod_a_ready, 1)
                    elif kind == "MT":
                        nc.scalar.activation(mod_b[:], mod_cols[:, b, 2 * DK:4 * DK], ACT.Copy).then_inc(mod_b_ready, 1)
                    elif kind == "SM":
                        tile = S[:, :, n * P:(n + 1) * P]
                        act.wait_ge(sub_done, T * b + n + 1)
                        nc.scalar.activation(tile, tile, ACT.Exp).then_inc(exp_done, 1)
                        act.wait_ge(exp_done, T * b + n + 1)
                        wait(act, av_done, T * b + max(n - RING + 1, 0))
                        nc.scalar.activation(Phi[:, n % RING, :, :], tile, ACT.Copy).then_inc(phi_done, 1)

            over_batches(act, part)

        @block.vector
        def _(dve):
            V_ = nc.vector
            V_.memset(half_power[:], -0.5).then_inc(const_ready, 1)
            V_.memset(V[:, :, D:D + 1].bitcast(F32), 1.0)
            V_.memset(V[:, :, D + 1:VW].bitcast(F32), 0.0)
            V_.memset(V[:, :, VW + D:VW + D + 1].bitcast(F32), 1.0)
            V_.memset(V[:, :, VW + D + 1:2 * VW].bitcast(F32), 0.0)
            dve.wait_ge(sig_step, 1)
            V_.tensor_scalar(sig1, sig, 1.0, None, ALU.add).then_inc(sig_step, 1)
            dve.wait_ge(sig_step, 2)
            V_.reciprocal(sig2, sig1).then_inc(sig_step, 1)
            dve.wait_ge(sig_step, 3)
            V_.tensor_tensor(siluT, cT_sb, sig2, ALU.mult).then_inc(silu_step, 1)
            dve.wait_ge(modT_mm, 1)
            modT = acc[:, 0, 0, 0:4 * DK * NB].rearrange("p (n b) -> p b n", b=NB)
            for n in range(4):
                blocks = slice(n * DK, (n + 1) * DK)
                V_.tensor_scalar(mod_cols[:, :, blocks], modT[:, :, blocks], 1.0 if n % 2 == 0 else 0.0, None, ALU.add).then_inc(modT_ready, 1)

            def mlp_weights():
                dve.wait_ge(w_hi_ready, 2)
                V_.tensor_tensor(W1lo[:], W1_sb, W1hi[:].bitcast(F32), ALU.subtract).then_inc(w_ready, 1)
                V_.tensor_tensor(W2lo[:], W2_sb, W2hi[:].bitcast(F32), ALU.subtract).then_inc(w_ready, 1)
                dve.wait_ge(pool_const, 5)
                V_.tensor_copy(select[:], select_sb).then_inc(w_ready, 2)

            def gates():
                dve.wait_ge(mod_mm, 1)
                V_.tensor_copy(mods[:, 0:2, :], score[0][0:NB, 0:2 * D].rearrange("p (a d) -> p a d", d=D)).then_inc(mod_step, 1)
                gates_ps = score[1][0:NB, :].rearrange("p (a d) -> p a d", d=HR)[:, :, 0:D]
                V_.tensor_copy(mods[:, 2:4, :], gates_ps).then_inc(mod_step, 1)
                dve.wait_ge(mod_step, 2)
                g = mods[:, 2:4, :]
                V_.tensor_scalar(signs, g, 0.0, 2.0, ALU.is_ge, ALU.mult).then_inc(mod_step, 1)
                V_.scalar_tensor_tensor(mags, g, -1.0, g, ALU.mult, ALU.max).then_inc(mod_step, 1)
                dve.wait_ge(mod_step, 4)
                V_.tensor_scalar(mags, mags, 0.25, None, ALU.max).then_inc(mod_step, 1)
                dve.wait_ge(mod_step, 5)
                V_.scalar_tensor_tensor(mags, signs, -1.0, mags, ALU.add, ALU.mult).then_inc(mod_step, 1)
                dve.wait_ge(mod_step, 6)
                dve.wait_ge(b2_in, 16)
                V_.scalar_tensor_tensor(mod_out[:, 0, :], mods[:, 1, :], 1.0, mags[:, 0, :], ALU.add, ALU.mult)
                V_.tensor_tensor(mod_out[:, 1, :], mods[:, 0, :], mags[:, 0, :], ALU.mult)
                V_.tensor_tensor(mod_out[:, 2, :], b2_sb, mags[:, 1, :], ALU.mult).then_inc(mods_ready, 1)

            def subtract_max(b, n):
                tile = S[:, :, n * P:(n + 1) * P]
                if n == 0:
                    dve.wait_ge(max_done, b + 1)
                most = max_ps[:, n * P:(n + 1) * P].unsqueeze(1).broadcast_to([P, T, P])
                V_.tensor_tensor(tile, tile, most, ALU.add).then_inc(sub_done, 1)

            def part(b, ph):
                f = b - 1
                features = ph.feature_base(b)
                for kind, n in ph.steps:
                    q = features + ph.jobs(FEATURE_JOBS, (kind, n))
                    if kind == "SC":
                        dve.wait_ge(scores_done, T * b + n + 1)
                        V_.tensor_scalar(S[:, n, :], score[n % 2][:], 1.0, None, ALU.mult, ALU.max,
                                         accum_out=row_max[:, n:n + 1]).then_inc(scores_read, 1)
                    elif kind == "MT":
                        dve.wait_ge(scores_read, T * b + T)
                        V_.tensor_scalar(neg_max[:, 0:T], row_max[:], -1.0, None, ALU.mult).then_inc(maxT_step, 1)
                        dve.wait_ge(maxT_step, 2 * b + 1)
                        V_.scalar_tensor_tensor(neg_max[:, T:2 * T], row_max[:], -1.0, neg_max[:, 0:T].bitcast(F32),
                                                ALU.mult, ALU.subtract).then_inc(maxT_step, 1)
                        dve.wait_ge(maxT_done, b + 1)
                        V_.tensor_copy(neg_maxT, maxT_ps).then_inc(maxT_ready, 1)
                    elif kind == "SM":
                        if n == 0:
                            subtract_max(b, 0)
                        if n + 1 < T:
                            subtract_max(b, n + 1)
                        dve.wait_ge(phi_done, T * b + n + 1)
                        V_.tensor_tensor(Plo[:, n % RING, :, :], S[:, :, n * P:(n + 1) * P],
                                         Phi[:, n % RING, :, :].bitcast(F32), ALU.subtract).then_inc(plo_done, 1)
                    elif kind == "AV":
                        e, product = T * b + n + 1, av_ps[n % 2][:, 0:D]
                        dve.wait_ge(av_done, e)
                        V_.reciprocal(inv_sum[:], av_ps[n % 2][:, D:D + 1]).then_inc(inv_ready, 1)
                        dve.wait_ge(inv_ready, e)
                        if n == 0:
                            dve.wait_ge(attn_mod_in, 16 * (b + 1))
                        V_.scalar_tensor_tensor(product, product, inv_sum[:], attn_mod[:, 0, :], ALU.mult, ALU.mult).then_inc(av_scaled, 1)
                        dve.wait_ge(av_scaled, e)
                        dve.wait_ge(xc_done, T // 2 * b + n // 2 + 1)
                        V_.tensor_tensor(x_cur[:, n, :], product, x_cur[:, n, :], ALU.add).then_inc(av_read, 1)
                        dve.wait_ge(av_read, e)
                        V_.bn_stats(stats[:, n % HT, :], x_cur[:, n, :]).then_inc(x2_stats, 1)
                        wait_apart(dve, x2_stats, e)
                        V_.bn_aggr(mv2[:, n, :], stats[:, n % HT, :]).then_inc(x2_mv, 1)
                    elif kind == "L1":
                        e = HT * (2 * b + 2 + n)
                        dve.wait_ge(ln1_in, 16 * (2 * b + n + 3))
                        for t in range(HT):
                            V_.bn_stats(stats1[:, t, :], ln1[:, t, :]).then_inc(ln1_stats, 1)
                        for t in range(HT):
                            wait_apart(dve, ln1_stats, e + t + 1)
                            V_.bn_aggr(mv1[:, n * HT + t, :], stats1[:, t, :]).then_inc(ln1_mv, 1)
                    elif kind == "V":
                        dve.wait_ge(v_ln, HT * (2 * b + n + 1))
                        wait(dve, av_done, T * b)
                        tiles = slice(n * HT, (n + 1) * HT)
                        V_.tensor_copy(V[:, tiles, VW:VW + D], ln1[:]).then_inc(v_hi, 1)
                        dve.wait_ge(v_hi, 2 * b + n + 1)
                        V_.tensor_tensor(V[:, tiles, 0:D], ln1[:], V[:, tiles, VW:VW + D].bitcast(F32), ALU.subtract).then_inc(v_done, 1)
                    elif kind in ("TH", "T2"):
                        cols = slice(n * HR, (n + 1) * HR)
                        for kk in range(DK):
                            dve.wait_ge(feat_hi, q + kk + 1)
                            if kind == "TH":
                                V_.scalar_tensor_tensor(Llo[:, kk, cols], featT[:, kk, :], wl[:, kk:kk + 1],
                                                        Lhi[:, kk, cols].bitcast(F32), ALU.mult, ALU.subtract)
                                V_.scalar_tensor_tensor(Rlo[:, kk, cols], featT[:, kk, :], wr[:, kk:kk + 1],
                                                        Rhi[:, kk, cols].bitcast(F32), ALU.mult, ALU.subtract).then_inc(feat_done, 1)
                            else:
                                V_.tensor_tensor(h2lo[:, kk, cols], featT[:, kk, :], h2hi[:, kk, cols].bitcast(F32),
                                                 ALU.subtract).then_inc(feat_done, 1)
                    elif kind == "OUT":
                        dve.wait_ge(acc_done, NF * f + FT * (n + 1))
                        if n == 0:
                            dve.wait_ge(gb_in, 16 * b)
                            dve.wait_ge(xg_done, T // 2 * b)
                        for a in range(2):
                            V_.tensor_tensor(acc[:, a, :, :], acc[:, a, :, :], gb_all[:].unsqueeze(1).broadcast_to([P, 2, D]),
                                             ALU.mult).then_inc(acc_mul, 1)
                        for a in range(2):
                            tiles = slice(n * HT + 2 * a, n * HT + 2 * a + 2)
                            dve.wait_ge(acc_mul, 4 * f + 2 * n + a + 1)
                            V_.tensor_tensor(x_mlp[:, tiles, :], acc[:, a, :, :], x_mlp[:, tiles, :], ALU.add).then_inc(out_done, 1)

            part(-1, PH["before"])
            mlp_weights()
            gates()
            part(0, PH["first"])
            with dve.Fori(1, NB - 1) as b:
                part(b, PH["middle"])
            part(NB - 1, PH["last"])
            part(NB, PH["after"])

        @block.gpsimd
        def _(pool):
            G = nc.gpsimd
            G.memset(ident[:], 0.0).then_inc(pool_const, 1)
            pool.wait_ge(pool_const, 1)
            G.affine_select(out=ident[:], in_=ident[:], compare_op=ALU.not_equal, fill=1.0, base=0,
                            pattern=[[-1, P]], channel_multiplier=1).then_inc(pool_const, 1)
            G.memset(select_sb, 0.0).then_inc(pool_const, 1)
            for copy in range(2):
                pool.wait_ge(pool_const, 3 + copy)
                G.affine_select(out=select_sb, in_=select_sb, compare_op=ALU.not_equal, fill=1.0, base=-T * copy,
                                pattern=[[-1, T], [0, P]], channel_multiplier=1).then_inc(pool_const, 1)
            pool.wait_ge(const_ready, 1)

            def normalise(out_tiles, in_tiles, mv, nm, rs, h, eps_done, rstd_done, count, done):
                tiles = slice(h * HT, (h + 1) * HT)
                G.tensor_scalar(nm[:, tiles], mv[:, tiles, 0], -1.0, 0.0, ALU.mult, ALU.add)
                G.tensor_scalar(var_eps[:], mv[:, tiles, 1], 1.0, EPS, ALU.mult, ALU.add).then_inc(eps_done, 1)
                pool.wait_ge(eps_done, count)
                G.tensor_tensor(rs[:, tiles], var_eps[:], half_power[:], ALU.pow).then_inc(rstd_done, 1)
                wait_apart(pool, rstd_done, count)
                for t in range(HT):
                    i = h * HT + t
                    last = G.tensor_scalar(out_tiles[:, t, :], in_tiles[:, t, :], nm[:, i:i + 1], rs[:, i:i + 1], ALU.add, ALU.mult)
                last.then_inc(done, 1)

            def part(b, ph):
                f = b - 1
                for kind, n in ph.steps:
                    if kind == "F":
                        pool.wait_ge(hid_hi_done, NF * f + n + 1)
                        G.tensor_tensor(hid_lo[:, n % RING, :], hid[:, n % 2, :], hid_hi[:, n % RING, :].bitcast(F32),
                                        ALU.subtract).then_inc(hid_lo_done, 1)
                    elif kind == "L1":
                        wait_apart(pool, ln1_mv, HT * (2 * b + 3 + n))
                        normalise(ln1, ln1, mv1, nm1, rs1, n, ln1_eps, ln1_rstd, 2 * b + 3 + n, ln1_done)
                    elif kind == "L2":
                        batch = b if n == 0 else f
                        wait_apart(pool, x2_mv, T * batch + HT * (n + 1))
                        normalise(ln2, x_cur[:, n * HT:(n + 1) * HT, :], mv2, nm2, rs2, n, ln2_eps, ln2_rstd, 2 * batch + n + 1, ln2_done)
                    elif kind == "VL":
                        pool.wait_ge(x_in[n], 16 * (b + 1))
                        if n == 0:
                            wait_apart(pool, feat_done, ph.feature_base(b))
                        else:
                            wait_apart(pool, v_done, 2 * b + 1)
                        for t in range(HT):
                            i = n * HT + t
                            G.tensor_scalar(ln1[:, t, :], x_cur[:, i, :], nm1[:, i:i + 1], rs1[:, i:i + 1], ALU.add, ALU.mult).then_inc(v_ln, 1)
                    elif kind == "XC":
                        if n == 0:
                            pool.wait_ge(attn_mod_in, 16 * (b + 1))
                        pair = x_cur[:, 2 * n:2 * n + 2, :]
                        pool.wait_ge(v_ln, HT * (2 * b + n // 2 + 1))
                        G.tensor_tensor(pair, pair, attn_mod[:, 1:2, :].broadcast_to([P, 2, D]), ALU.add).then_inc(xc_done, 1)
                    elif kind == "XG":
                        batch = b if n < 2 else f
                        if n in (0, 2):
                            wait(pool, stored[n // 2], 16 * (batch + n // 2))
                            pool.wait_ge(gb_b2_in, 16 * (batch + 1))
                        G.tensor_tensor(x_mlp[:, 2 * n:2 * n + 2, :], x_cur[:, 2 * n:2 * n + 2, :],
                                        gb_b2[:].unsqueeze(1).broadcast_to([P, 2, D]), ALU.add).then_inc(xg_done, 1)

            over_batches(pool, part)


def kernel(L0_attn_x, L0_attn_w_lhs, L0_attn_w_rhs, L0_ffn_W1, L0_ffn_b1, L0_ffn_W2, L0_ffn_b2, L0_c, L0_wmod):
    import numpy as np
    import concourse.bacc as bacc
    from concourse.bass_utils import run_bass_kernel_spmd

    def by_feature(v):
        return np.ascontiguousarray(np.asarray(v).reshape(-1, P).T)

    arrays = {
        "x": np.ascontiguousarray(L0_attn_x),
        "w_lhs": by_feature(L0_attn_w_lhs),
        "w_rhs": by_feature(L0_attn_w_rhs),
        "W1": np.ascontiguousarray(L0_ffn_W1),
        "b1": by_feature(L0_ffn_b1),
        "W2": np.ascontiguousarray(L0_ffn_W2),
        "b2": np.ascontiguousarray(L0_ffn_b2),
        "cT": np.ascontiguousarray(np.asarray(L0_c).T),
        "wmod": np.ascontiguousarray(L0_wmod),
    }
    nc = bacc.Bacc("TRN2", target_bir_lowering=False, num_devices=1)
    args = [nc.dram_tensor(name, a.shape, mybir.dt.from_np(a.dtype), kind="ExternalInput").ap() for name, a in arrays.items()]
    out = nc.dram_tensor("out", arrays["x"].shape, F32, kind="ExternalOutput").ap()
    block_kernel(nc, *args, out)
    result = run_bass_kernel_spmd(nc, [arrays], core_ids=[0])
    return result.results[0]["out"]
```

```python
from contextlib import ExitStack

import concourse.bass as bass
from concourse import mybir

F32 = mybir.dt.float32
F32R = mybir.dt.float32r
ALU = mybir.AluOpType
ACT = mybir.ActivationFunctionType

P = 128
EPS = 1e-5

STEPS = {
    "pe": """
        SC.0 F.0- F.1- SC.1 SC.2 SC.3 T2.1- SC.4 F.2- SC.5 F.3- F.4- G.0- G.1- SC.6 SC.7 F.5- G.2- G.3- MT.0
        F.6- MB.0 G.4- F.7- F.8- G.5- G.6- F.9- AV.0 G.7- TH.0+ AV.1 F.10- F.11- G.8- F.12- AV.2 G.9- AV.3
        G.10- TH.1+ AV.4 F.13- G.11- AV.5 F.14- F.15- T2.0 G.12- AV.6 AV.7 G.13- G.14- G.15-
    """,
    "act": """
        F.0- F.1- T2.1- F.2- F.3- F.4- MT.0 F.5- F.6- EX.0 F.7- EX.1 SM.0 SM.1 F.8- F.9- L1.0+ EX.2 SM.2
        EX.3 TH.0+ SM.3 F.10- EX.4 SM.4 F.11- F.12- EX.5 EX.6 SM.5 TH.1+ SM.6 EX.7 F.13- SM.7 F.14- F.15-
        T2.0
    """,
    "dve": """
        SC.0 SC.1 SC.2 SC.3 SC.4 V.0 T2.1- SC.5 SC.6 SC.7 MT.0 V.1 SB.0 SB.1 SB.2 L1.0+ SM.0 SM.1 SB.3 SB.4
        AV.0 OUT.0- AV.1 SM.2 SM.3 L1.1+ SB.5 SB.6 SB.7 AV.2 TH.0+ SM.4 AV.3 SM.5 TH.1+ SM.6 SM.7 AV.4 AV.5
        AV.6 T2.0 AV.7 OUT.1-
    """,
    "pool": """
        N2.1- F.0- VL.0 XG.2- XG.3- F.1- F.2- F.3- F.4- XC.0 VL.1 XC.1 XC.2 XC.3 F.5- F.6- L1.0+ F.7- N1.0+
        F.8- F.9- F.10- F.11- L1.1+ N1.1+ L2.0 F.12- F.13- N2.0 XG.0 F.14- XG.1 F.15- L2.1
    """,
}
BEFORE_STEPS = {
    "pe": """
        TH.0+ MF.0+ TH.1+
    """,
    "act": """
        L1.0+ TH.0+ TH.1+
    """,
    "dve": """
        L1.0+ SI.0+ L1.1+ MA.0+ TH.0+ TH.1+ MF.0+
    """,
    "pool": """
        L1.0+ N1.0+ L1.1+ N1.1+ TH.0+ TH.1+
    """,
}
FIRST_STEPS = {
    "pe": """
        SC.0 SC.1 MD.0 SC.2 SC.3 SC.4 SC.5 SC.6 SC.7 MT.0 MB.0 AV.0 AV.1 TH.0+ AV.2 AV.3 TH.1+ AV.4 T2.0
        AV.5 AV.6 AV.7
    """,
    "act": """
        WS.0 EX.0 EX.1 MT.0 SM.0 SM.1 EX.2 SM.2 EX.3 L1.0+ SM.3 TH.0+ EX.4 SM.4 EX.5 SM.5 TH.1+ EX.6 SM.6
        EX.7 SM.7 T2.0
    """,
    "dve": """
        SC.0 SC.1 GA.0 SC.2 SC.3 SC.4 V.0 SC.5 SC.6 SC.7 MT.0 V.1 SB.0 SB.1 SB.2 L1.0+ SM.0 SM.1 SM.2 SB.3
        SB.4 AV.0 SM.3 AV.1 TH.0+ L1.1+ AV.2 SB.5 SB.6 AV.3 SM.4 SM.5 TH.1+ SB.7 SM.6 AV.4 SM.7 AV.5 T2.0
        AV.6 AV.7
    """,
    "pool": """
        WS.0 VL.0 XC.0 XC.1 VL.1 XC.2 L1.0+ XC.3 N1.0+ L1.1+ N1.1+ L2.0 N2.0 L2.1 XG.0 XG.1
    """,
}


class Phase:

    def __init__(self, orders, which, col_base, feature_base):
        suffixes = {"-": "prev", "+": "next"}
        self.steps = {}
        for engine, order in orders.items():
            self.steps[engine] = []
            for step in order.split():
                if suffixes.get(step[-1], "this") in which:
                    kind, number = step.rstrip("+-").split(".")
                    self.steps[engine].append((kind, int(number)))
        self.has = which
        self.col_base = col_base
        self.feature_base = feature_base

    def jobs(self, weights, until=None):
        total = 0
        for step in self.steps["pe"]:
            if step == until:
                break
            total += weights.get(step[0], 0)
        return total


COL_JOBS = {"F": 1, "T2": 2, "TH": 2}
FEATURE_JOBS = {"T2": 2, "TH": 2}


def phases(NB):
    made = {}

    def add(name, which, col_base, feature_base, steps=STEPS):
        made[name] = Phase(steps, which, col_base, feature_base)
        return made[name].jobs(COL_JOBS), made[name].jobs(FEATURE_JOBS)

    c0, f0 = add("before", {"next"}, lambda b: 0, lambda b: 0, BEFORE_STEPS)
    c1, f1 = add("first", {"this", "next"}, lambda b: c0, lambda b: f0, FIRST_STEPS)
    c1, f1 = c0 + c1, f0 + f1
    cm, fm = add("middle", {"prev", "this", "next"}, lambda b: b * cm + (c1 - cm), lambda b: b * fm + (f1 - fm))
    cl, fl = add("last", {"prev", "this"}, lambda b: c1 + (NB - 2) * cm, lambda b: f1 + (NB - 2) * fm)
    add("after", {"prev"}, lambda b: c1 + (NB - 2) * cm + cl, lambda b: f1 + (NB - 2) * fm + fl)
    return made


def block_kernel(nc, x, w_lhs, w_rhs, W1, b1, W2, b2, cT, wmod, out):
    NB, ROWS, D = x.shape
    FF = W1.shape[1]
    T = ROWS // P
    DK = D // P
    FT = FF // P
    HR = ROWS // 2
    HT = T // 2
    RING = 3
    VW = D + 2
    assert T == 8 and DK == 2 and FT == 8 and HR == 512 and NB >= 3
    NF = 2 * FT

    first_col = [P * j for j in range(T)]
    first_col[3], first_col[7] = 2 * P, 6 * P

    PH = phases(NB)
    rows = lambda b, h, dram: dram[b, h * HR:(h + 1) * HR, :].rearrange("(t p) d -> p t d", p=P)
    x_rows = x.rearrange("b (h t p) d -> b h p t d", p=P, h=2)
    out_rows = out.rearrange("b (h t p) d -> b h p t d", p=P, h=2)
    mod_rows = nc.dram_tensor("mod_rows", [NB, 4, D], F32, kind="Internal").ap()

    with ExitStack() as ctx:
        sb = lambda name, shape, dt=F32: ctx.enter_context(nc.sbuf_tensor(name, shape, dt))
        psum = lambda name, shape: ctx.enter_context(nc.psum_tensor(name, shape, F32))
        sem = lambda name: ctx.enter_context(nc.semaphore(name))

        ident = sb("ident", [P, P])
        select = sb("select", [2 * T, T, P], F32R)
        W1hi, W1lo = sb("W1hi", [P, DK, FF], F32R), sb("W1lo", [P, DK, FF], F32R)
        W2hi, W2lo = sb("W2hi", [P, FT, D], F32R), sb("W2lo", [P, FT, D], F32R)
        b1T = sb("b1T", [P, FT])
        wl, wr = sb("wl", [P, DK]), sb("wr", [P, DK])
        mod_cols = sb("mod_cols", [P, NB, 4 * DK])
        mod_a, mod_b = sb("mod_a", [P, 2 * DK]), sb("mod_b", [P, 2 * DK])
        attn_mod, gb_b2, gb_all = sb("attn_mod", [P, 2, D]), sb("gb_b2", [P, D]), sb("gb_all", [P, D])
        S = sb("S", [P, T, ROWS])
        Phi, Plo = sb("Phi", [P, RING, T, P], F32R), sb("Plo", [P, RING, T, P], F32R)
        Lhi, Llo = sb("Lhi", [P, DK, ROWS], F32R), sb("Llo", [P, DK, ROWS], F32R)
        Rhi, Rlo = sb("Rhi", [P, DK, ROWS], F32R), sb("Rlo", [P, DK, ROWS], F32R)
        V = sb("V", [P, T, 2 * VW], F32R)
        x_cur = sb("x_cur", [P, T, D])
        x_mlp = sb("x_mlp", [P, T, D])
        ln1, ln2 = sb("ln1", [P, HT, D]), sb("ln2", [P, HT, D])
        featT = sb("featT", [P, DK, HR])
        hid = sb("hid", [P, 2, HR])
        hid_hi, hid_lo = sb("hid_hi", [P, RING, HR], F32R), sb("hid_lo", [P, RING, HR], F32R)
        h2hi, h2lo = sb("h2hi", [P, DK, ROWS], F32R), sb("h2lo", [P, DK, ROWS], F32R)
        stats, stats1 = sb("stats", [P, HT, 6]), sb("stats1", [P, HT, 6])
        mv1, nm1, rs1 = sb("mv1", [P, T, 2]), sb("nm1", [P, T]), sb("rs1", [P, T])
        mv2, nm2, rs2 = sb("mv2", [P, T, 2]), sb("nm2", [P, T]), sb("rs2", [P, T])
        var_eps, half_power = sb("var_eps", [P, HT]), sb("half_power", [P, HT])
        row_max, neg_max = sb("row_max", [P, T]), sb("neg_max", [P, 2 * T], F32R)
        neg_maxT = Phi[0:2 * T, RING - 1, 0, :]
        inv_sum = sb("inv_sum", [P, 1])

        wmod_a = S[:, 7, :].rearrange("p (k n) -> p k n", k=DK)
        wmod_b = x_mlp[:].rearrange("p (k m) d -> p k (m d)", k=DK)
        W1_sb = S[:, 3:5, :]
        W2_sb = S[:, 5:7, :].rearrange("p a (i d) -> p (a i) d", d=D)
        select_sb = S[0:2 * T, 2, :].rearrange("p (j c) -> p j c", c=P)
        cT_sb = hid[:, 0, 0:DK * NB].rearrange("p (k b) -> p k b", b=NB)
        siluT = hid[:, 0, 64:64 + DK * NB].rearrange("p (k b) -> p k b", b=NB)
        sig = hid[:, 1, 0:DK * NB].rearrange("p (k b) -> p k b", b=NB)
        sig1 = hid[:, 1, 64:64 + DK * NB].rearrange("p (k b) -> p k b", b=NB)
        sig2 = hid[:, 1, 128:128 + DK * NB].rearrange("p (k b) -> p k b", b=NB)
        mods = ln2[0:NB, :, :]
        signs = featT[0:NB, 0, :].rearrange("p (a d) -> p a d", d=D)
        mags = featT[0:NB, 1, :].rearrange("p (a d) -> p a d", d=D)
        attn_out = hid[0:NB, 1, :].rearrange("p (a d) -> p a d", d=D)
        mlp_out = hid[0:NB, 0, :].rearrange("p (a d) -> p a d", d=D)
        b2_sb = mlp_out[:, 1, :]

        score = [psum("score0", [P, ROWS]), psum("score1", [P, ROWS])]
        col = [psum("col0", [P, HR]), psum("col1", [P, HR])]
        acc = psum("acc", [P, 2, 2, D])
        acc_modT = acc[:, 0, 0, 0:4 * DK * NB]
        maxT_ps = score[0][0:2 * T, 0:P]
        max_ps = score[1]
        av_ps = [score[0][:, 0:VW], score[0][:, HR:HR + VW]]

        c_in, small_in, b2_in = sem("c_in"), sem("small_in"), sem("b2_in")
        wmod_a_in, wmod_b_in, w_in = sem("wmod_a_in"), sem("wmod_b_in"), sem("w_in")
        mods_stored = sem("mods_stored")
        ln1_in = sem("ln1_in")
        x_in = [sem("x_in0"), sem("x_in1")]
        attn_mod_in, gb_b2_in, gb_in = sem("attn_mod_in"), sem("gb_b2_in"), sem("gb_in")
        stored = [sem("stored0"), sem("stored1")]
        passed = sem("passed")
        const_ready, pool_const = sem("const_ready"), sem("pool_const")
        silu_step, sig_step = sem("silu_step"), sem("sig_step")
        modT_mm, mod_mm, mod_step = sem("modT_mm"), sem("mod_mm"), sem("mod_step")
        modT_ready, mods_ready = sem("modT_ready"), sem("mods_ready")
        w_hi_ready, w_ready = sem("w_hi_ready"), sem("w_ready")
        scores_done, scores_read = sem("scores_done"), sem("scores_read")
        maxT_step, maxT_done, maxT_ready, max_done = sem("maxT_step"), sem("maxT_done"), sem("maxT_ready"), sem("max_done")
        sub_done, exp_done, phi_done, plo_done = sem("sub_done"), sem("exp_done"), sem("phi_done"), sem("plo_done")
        rhi_done = sem("rhi_done")
        av_done, av_read, inv_ready = sem("av_done"), sem("av_read"), sem("inv_ready")
        av_scaled, x2_stats, x2_mv = sem("av_scaled"), sem("x2_stats"), sem("x2_mv")
        xc_done, xg_done = sem("xc_done"), sem("xg_done")
        ln1_stats, ln1_mv, ln1_eps, ln1_rstd, ln1_done = sem("ln1_stats"), sem("ln1_mv"), sem("ln1_eps"), sem("ln1_rstd"), sem("ln1_done")
        ln2_eps, ln2_rstd, ln2_done = sem("ln2_eps"), sem("ln2_rstd"), sem("ln2_done")
        v_ln, v_hi, v_done = sem("v_ln"), sem("v_hi"), sem("v_done")
        col_done, col_read = sem("col_done"), sem("col_read")
        mod_a_ready, mod_b_ready = sem("mod_a_ready"), sem("mod_b_ready")
        feat_hi, feat_done = sem("feat_hi"), sem("feat_done")
        hid_hi_done, hid_lo_done = sem("hid_hi_done"), sem("hid_lo_done")
        acc_done, acc_mul, out_done = sem("acc_done"), sem("acc_mul"), sem("out_done")

        def wait(eng, semaphore, value):
            if not (isinstance(value, int) and value <= 0):
                eng.wait_ge(semaphore, value)

        def wait_apart(eng, semaphore, value):
            eng.wait_ge(semaphore, value)
            eng.sem_inc(passed, 1)

        def over_batches(eng, part):
            part(-1, PH["before"])
            part(0, PH["first"])
            with eng.Fori(1, NB - 1) as b:
                part(b, PH["middle"])
            part(NB - 1, PH["last"])
            part(NB, PH["after"])

        block = ctx.enter_context(nc.Block())

        @block.sync
        def _(sp):
            sp.sem_inc(stored[1], 16)
            wmod_rows = wmod.rearrange("(k p) n -> p k n", p=P)
            sp.dma_start(cT_sb, cT.rearrange("(k p) b -> p k b", p=P)).then_inc(c_in, 16)
            sp.dma_start(x_cur[:, 0:HT, :], x_rows[0, 0]).then_inc(x_in[0], 16)
            sp.dma_start(wmod_a, wmod_rows[:, :, 0:2 * D]).then_inc(wmod_a_in, 16)
            sp.dma_start(wl[:], w_lhs).then_inc(small_in, 16)
            sp.dma_start(wr[:], w_rhs).then_inc(small_in, 16)
            sp.dma_start(x_cur[:, HT:T, :], x_rows[0, 1]).then_inc(x_in[1], 16)
            sp.dma_start(wmod_b, wmod_rows[:, :, 2 * D:6 * D]).then_inc(wmod_b_in, 16)
            sp.dma_start(b1T[:], b1).then_inc(small_in, 16)
            sp.dma_start(b2_sb, b2.partition_broadcast(NB)).then_inc(b2_in, 16)
            sp.dma_start(W1_sb, W1.rearrange("(k p) n -> p k n", p=P)).then_inc(w_in, 16)
            sp.dma_start(W2_sb, W2.rearrange("(i p) d -> p i d", p=P)).then_inc(w_in, 16)
            sp.wait_ge(mods_ready, 1)
            sp.dma_start(mod_rows[:, 0:2, :], attn_out).then_inc(mods_stored, 16)
            sp.dma_start(mod_rows[:, 2:4, :], mlp_out).then_inc(mods_stored, 16)
            sp.wait_ge(mods_stored, 32)

            def part(b, ph):
                f = b - 1
                if "this" in ph.has:
                    wait(sp, av_read, T * b)
                    sp.dma_start(attn_mod[:].rearrange("p a d -> p (a d)"),
                                 mod_rows[b, 0:2, :].rearrange("a d -> (a d)").partition_broadcast(P)).then_inc(attn_mod_in, 16)
                if "prev" in ph.has:
                    sp.dma_start(gb_all[:], mod_rows[f, 2, :].partition_broadcast(P)).then_inc(gb_in, 16)
                if "this" in ph.has:
                    if ph is not PH["first"]:
                        sp.wait_ge(xg_done, T // 2 * b)
                        sp.dma_start(x_cur[:, HT:T, :], x_rows[b, 1]).then_inc(x_in[1], 16)
                    sp.dma_start(gb_b2[:], mod_rows[b, 3, :].partition_broadcast(P)).then_inc(gb_b2_in, 16)
                if "next" in ph.has:
                    sp.wait_ge(v_done, 2 * b + 2)
                    sp.dma_start(ln1[:], x_rows[b + 1, 0]).then_inc(ln1_in, 16)
                if "prev" in ph.has:
                    sp.wait_ge(out_done, 4 * f + 2)
                    sp.dma_start(out_rows[f, 0], x_mlp[:, 0:HT, :]).then_inc(stored[0], 16)
                if "next" in ph.has:
                    sp.wait_ge(col_done, ph.col_base(b) + ph.jobs(COL_JOBS, ("TH", 0)) + DK)
                    sp.dma_start(ln1[:], x_rows[b + 1, 1]).then_inc(ln1_in, 16)
                    sp.wait_ge(xg_done, T // 2 * b + 2)
                    sp.dma_start(x_cur[:, 0:HT, :], x_rows[b + 1, 0]).then_inc(x_in[0], 16)
                if "prev" in ph.has:
                    sp.wait_ge(out_done, 4 * f + 4)
                    sp.dma_start(out_rows[f, 1], x_mlp[:, HT:T, :]).then_inc(stored[1], 16)

            part(0, PH["first"])
            with sp.Fori(1, NB - 1) as b:
                part(b, PH["middle"])
            part(NB - 1, PH["last"])
            part(NB, PH["after"])
            for h in range(2):
                sp.wait_ge(stored[h], 16 * (NB + h))

        @block.tensor
        def _(pe):
            def wmod_part(kk, m, start, width):
                staged, at = (wmod_a, m * D) if m < 2 else (wmod_b, (m - 2) * D)
                return staged[:, kk, at + start:at + start + width]

            def modulation_by_feature(blocks, modT):
                for n in blocks:
                    m = (1, 0, 4, 3)[n]
                    for k in range(DK):
                        for kk in range(DK):
                            last = nc.tensor.matmul(modT[:, (n * DK + k) * NB:(n * DK + k + 1) * NB],
                                                    wmod_part(kk, m, k * P, P), siluT[:, kk, :],
                                                    start=(kk == 0), stop=(kk == DK - 1))
                last.then_inc(modT_mm, 1)

            pe.wait_ge(silu_step, 1)
            pe.wait_ge(wmod_a_in, 16)
            modulation_by_feature((0, 1), score[1][:, 0:4 * DK * NB])

            def modulation_by_row():
                pe.wait_ge(modT_ready, 4)
                for bank, at, m, width in ((0, 0, 0, 2), (1, 0, 2, 1), (1, 1, 5, 1)):
                    for kk in range(DK):
                        last = nc.tensor.matmul(acc[0:NB, bank, at:at + width, :], siluT[:, kk, :],
                                                wmod_part(kk, m, 0, width * D), start=(kk == 0), stop=(kk == DK - 1))
                last.then_inc(mod_mm, 1)

            def part(b, ph):
                f = b - 1
                column, features = ph.col_base(b), ph.feature_base(b)

                def second_layer(i):
                    slot, it = i % RING, i % FT
                    pe.wait_ge(hid_hi_done, NF * f + i + 1)
                    if i == 0:
                        pe.wait_ge(xg_done, T // 2 * f + T // 2)
                    elif it == 0:
                        pe.wait_ge(out_done, 4 * f + 2)
                    for t in range(HT):
                        o, hi = acc[:, t // 2, t % 2, :], hid_hi[:, slot, t * P:(t + 1) * P]
                        nc.tensor.matmul(o, hi, W2hi[:, it, :], start=(it == 0 and t % 2 == 0), stop=False, skip_group_check=True)
                        nc.tensor.matmul(o, hi, W2lo[:, it, :], start=False, stop=False, skip_group_check=True)
                    pe.wait_ge(hid_lo_done, NF * f + i + 1)
                    for t in range(HT):
                        o, lo = acc[:, t // 2, t % 2, :], hid_lo[:, slot, t * P:(t + 1) * P]
                        last = nc.tensor.matmul(o, lo, W2hi[:, it, :], start=False, stop=(it == FT - 1), skip_group_check=True)
                    last.then_inc(acc_done, 1)

                for kind, n in ph.steps["pe"]:
                    c = column + ph.jobs(COL_JOBS, (kind, n))
                    cb = ph.jobs(COL_JOBS, (kind, n)) % 2
                    if kind == "SC":
                        if n == 0:
                            pe.wait_ge(feat_done, features - DK if ph is PH["first"] else features)
                            wait(pe, av_read, T * b)
                        elif ph is PH["first"] and n == 1:
                            pe.wait_ge(modT_ready, 2)
                        elif n == 1:
                            pe.wait_ge(sub_done, T * b)
                        else:
                            pe.wait_ge(scores_read, T * b + n - 1)
                        at = first_col[n]
                        for lo_col in range(0, ROWS, HR):
                            start_col = max(at, lo_col)
                            width = lo_col + HR - start_col
                            if width <= 0:
                                continue
                            if ph is PH["first"] and n == 0 and lo_col > 0:
                                pe.wait_ge(feat_done, features)
                            o = score[n % 2][:, start_col:lo_col + HR]
                            tile, cols = slice(n * P, (n + 1) * P), slice(start_col, lo_col + HR)
                            for kk in range(DK):
                                nc.tensor.matmul(o, Lhi[:, kk, tile], Rhi[:, kk, cols], start=(kk == 0), stop=False)
                                nc.tensor.matmul(o, Lhi[:, kk, tile], Rlo[:, kk, cols], start=False, stop=False)
                                last = nc.tensor.matmul(o, Llo[:, kk, tile], Rhi[:, kk, cols], start=False, stop=(kk == DK - 1))
                        for i in range(at // P):
                            if i == at // P - 1:
                                pe.wait_ge(scores_read, T * b + i + 1)
                            last = nc.tensor.transpose(score[n % 2][:, i * P:(i + 1) * P], S[:, i, n * P:(n + 1) * P], ident[:])
                        last.then_inc(scores_done, 1)
                    elif kind == "F":
                        half, it = n // FT, n % FT
                        if it == 0:
                            pe.wait_ge(feat_done, features + DK * half)
                        pe.wait_ge(col_read, c - 1)
                        tile, cols = slice(it * P, (it + 1) * P), slice(half * HR, (half + 1) * HR)
                        for kk in range(DK):
                            nc.tensor.matmul(col[cb][:], W1hi[:, kk, tile], h2hi[:, kk, cols], start=(kk == 0), stop=False)
                            nc.tensor.matmul(col[cb][:], W1hi[:, kk, tile], h2lo[:, kk, cols], start=False, stop=False)
                            last = nc.tensor.matmul(col[cb][:], W1lo[:, kk, tile], h2hi[:, kk, cols], start=False, stop=(kk == DK - 1))
                        last.then_inc(col_done, 1)
                    elif kind == "G":
                        second_layer(n)
                    elif kind == "MF":
                        pe.wait_ge(wmod_b_in, 16)
                        modulation_by_feature((2, 3), acc_modT)
                    elif kind == "MD":
                        modulation_by_row()
                    elif kind in ("TH", "T2"):
                        if kind == "TH":
                            pe.wait_ge(ln1_done, 2 * (b + 1) + n + 1)
                            ln = ln2 if ph is PH["before"] and n == 1 else ln1
                            if ph is PH["before"] and n == 0:
                                pe.wait_ge(pool_const, 2)
                        else:
                            pe.wait_ge(ln2_done, 2 * (b if n == 0 else f) + n + 1)
                            ln = ln2
                        for kk in range(DK):
                            wait(pe, col_read, c + kk - 1)
                            for t in range(HT):
                                last = nc.tensor.transpose(col[(cb + kk) % 2][:, t * P:(t + 1) * P], ln[:, t, kk * P:(kk + 1) * P], ident[:])
                            last.then_inc(col_done, 1)
                    elif kind == "MT":
                        if ph is PH["first"]:
                            pe.wait_ge(w_ready, 4)
                        pe.wait_ge(maxT_step, 2 * b + 2)
                        nc.tensor.transpose(maxT_ps, neg_max[:].bitcast(F32), ident[:]).then_inc(maxT_done, 1)
                    elif kind == "MB":
                        pe.wait_ge(maxT_ready, b + 1)
                        for j in range(T):
                            last = nc.tensor.matmul(max_ps[:, j * P:(j + 1) * P], select[:, j, :], neg_maxT, start=True, stop=True)
                        last.then_inc(max_done, 1)
                    elif kind == "AV":
                        pe.wait_ge(phi_done, T * b + n + 1)
                        if n == 0:
                            pe.wait_ge(v_done, 2 * b + 2)
                        if n >= 2:
                            pe.wait_ge(av_read, T * b + n - 1)
                        slot, o = n % RING, av_ps[n % 2]
                        for t in range(T):
                            nc.tensor.matmul(o, Phi[:, slot, t, :], V[:, t, 0:VW], start=(t == 0), stop=False)
                            nc.tensor.matmul(o[:, 0:D], Phi[:, slot, t, :], V[:, t, VW:VW + D], start=False, stop=False)
                        pe.wait_ge(plo_done, T * b + n + 1)
                        for t in range(T):
                            last = nc.tensor.matmul(o, Plo[:, slot, t, :], V[:, t, VW:2 * VW], start=False, stop=(t == T - 1))
                        last.then_inc(av_done, 1)

            over_batches(pe, part)

        @block.scalar
        def _(act):
            act.wait_ge(c_in, 16)
            nc.scalar.activation(sig, cT_sb, ACT.Exp, scale=-1.0).then_inc(sig_step, 1)

            def part(b, ph):
                f = b - 1
                column, features = ph.col_base(b), ph.feature_base(b)
                for kind, n in ph.steps["act"]:
                    c = column + ph.jobs(COL_JOBS, (kind, n))
                    cb = ph.jobs(COL_JOBS, (kind, n)) % 2
                    q = features + ph.jobs(FEATURE_JOBS, (kind, n))
                    if kind == "F":
                        act.wait_ge(col_done, c + 1)
                        if n >= 2:
                            act.wait_ge(hid_lo_done, NF * f + n - 1)
                        nc.scalar.activation(hid[:, n % 2, :], col[cb][:], ACT.Relu, bias=b1T[:, n % FT:n % FT + 1]).then_inc(col_read, 1)
                        act.wait_ge(col_read, c + 1)
                        if n >= RING:
                            act.wait_ge(acc_done, NF * f + n - RING + 1)
                        nc.scalar.activation(hid_hi[:, n % RING, :], hid[:, n % 2, :], ACT.Copy).then_inc(hid_hi_done, 1)
                    elif kind in ("TH", "T2"):
                        half = n
                        mod = mod_a if kind == "TH" else mod_b
                        if kind == "TH":
                            act.wait_ge(mod_a_ready, b + 2)
                        else:
                            act.wait_ge(mod_b_ready, (b if n == 0 else f) + 1)
                        cols = slice(half * HR, (half + 1) * HR)
                        for kk in range(DK):
                            act.wait_ge(col_done, c + kk + 1)
                            wait(act, feat_done, q + kk - 1)
                            nc.scalar.activation(featT[:, kk, :], col[(cb + kk) % 2][:], ACT.Identity,
                                                 scale=mod[:, kk:kk + 1], bias=mod[:, DK + kk:DK + kk + 1]).then_inc(col_read, 1)
                            act.wait_ge(col_read, c + kk + 1)
                            if kind == "TH":
                                last = nc.scalar.activation(Lhi[:, kk, cols], featT[:, kk, :], ACT.Copy, scale=wl[:, kk:kk + 1])
                                if ph is not PH["before"]:
                                    last = nc.scalar.activation(Rhi[:, kk, cols], featT[:, kk, :], ACT.Copy, scale=wr[:, kk:kk + 1])
                                last.then_inc(feat_hi, 1)
                            else:
                                nc.scalar.activation(h2hi[:, kk, cols], featT[:, kk, :], ACT.Copy).then_inc(feat_hi, 1)
                    elif kind == "WS":
                        act.wait_ge(w_in, 32)
                        nc.scalar.activation(W1hi[:], W1_sb, ACT.Copy).then_inc(w_hi_ready, 1)
                        nc.scalar.activation(W2hi[:], W2_sb, ACT.Copy).then_inc(w_hi_ready, 1)
                    elif kind == "L1" and n == 0:
                        if ph is PH["before"]:
                            act.wait_ge(modT_ready, 2)
                            act.wait_ge(small_in, 48)
                        nc.scalar.activation(mod_a[:], mod_cols[:, b + 1, 0:2 * DK], ACT.Copy).then_inc(mod_a_ready, 1)
                    elif kind == "MT":
                        if ph is PH["first"]:
                            act.wait_ge(modT_ready, 4)
                        nc.scalar.activation(mod_b[:], mod_cols[:, b, 2 * DK:4 * DK], ACT.Copy).then_inc(mod_b_ready, 1)
                    elif kind == "EX":
                        tile = S[:, :, n * P:(n + 1) * P]
                        act.wait_ge(sub_done, T * b + n + 1)
                        nc.scalar.activation(tile, tile, ACT.Exp).then_inc(exp_done, 1)
                    elif kind == "SM":
                        act.wait_ge(exp_done, T * b + n + 1)
                        wait(act, av_done, T * b + max(n - RING + 1, 0))
                        nc.scalar.activation(Phi[:, n % RING, :, :], S[:, :, n * P:(n + 1) * P], ACT.Copy).then_inc(phi_done, 1)

            over_batches(act, part)

        @block.vector
        def _(dve):
            V_ = nc.vector
            V_.memset(half_power[:], -0.5).then_inc(const_ready, 1)
            V_.memset(V[:, :, D:D + 1].bitcast(F32), 1.0)
            V_.memset(V[:, :, D + 1:VW].bitcast(F32), 0.0)
            V_.memset(V[:, :, VW + D:VW + D + 1].bitcast(F32), 1.0)
            V_.memset(V[:, :, VW + D + 1:2 * VW].bitcast(F32), 0.0)

            def silu():
                dve.wait_ge(sig_step, 1)
                V_.tensor_scalar(sig1, sig, 1.0, None, ALU.add).then_inc(sig_step, 1)
                dve.wait_ge(sig_step, 2)
                V_.reciprocal(sig2, sig1).then_inc(sig_step, 1)
                dve.wait_ge(sig_step, 3)
                V_.tensor_tensor(siluT, cT_sb, sig2, ALU.mult).then_inc(silu_step, 1)

            def modulation_by_feature(blocks, modT):
                modT = modT.rearrange("p (n b) -> p b n", b=NB)
                for n in blocks:
                    cols = slice(n * DK, (n + 1) * DK)
                    V_.tensor_scalar(mod_cols[:, :, cols], modT[:, :, cols], 1.0 if n % 2 == 0 else 0.0, None, ALU.add).then_inc(modT_ready, 1)

            def gates():
                dve.wait_ge(mod_mm, 1)
                for bank in range(2):
                    V_.tensor_copy(mods[:, 2 * bank:2 * bank + 2, :], acc[0:NB, bank, :, :]).then_inc(mod_step, 1)
                dve.wait_ge(mod_step, 2)
                g = mods[:, 2:4, :]
                V_.tensor_scalar(signs, g, 0.0, 2.0, ALU.is_ge, ALU.mult).then_inc(mod_step, 1)
                V_.scalar_tensor_tensor(mags, g, -1.0, g, ALU.mult, ALU.max).then_inc(mod_step, 1)
                dve.wait_ge(mod_step, 4)
                V_.tensor_scalar(mags, mags, 0.25, None, ALU.max).then_inc(mod_step, 1)
                dve.wait_ge(mod_step, 5)
                ga, gb = mags[:, 0, :], mlp_out[:, 0, :]
                V_.scalar_tensor_tensor(ga, signs[:, 0, :], -1.0, ga, ALU.add, ALU.mult).then_inc(mod_step, 1)
                V_.scalar_tensor_tensor(gb, signs[:, 1, :], -1.0, mags[:, 1, :], ALU.add, ALU.mult).then_inc(mod_step, 1)
                dve.wait_ge(mod_step, 7)
                dve.wait_ge(b2_in, 16)
                V_.scalar_tensor_tensor(attn_out[:, 0, :], mods[:, 1, :], 1.0, ga, ALU.add, ALU.mult)
                V_.tensor_tensor(attn_out[:, 1, :], mods[:, 0, :], ga, ALU.mult)
                V_.tensor_tensor(b2_sb, b2_sb, gb, ALU.mult).then_inc(mods_ready, 1)

            def part(b, ph):
                f = b - 1
                features = ph.feature_base(b)
                for kind, n in ph.steps["dve"]:
                    q = features + ph.jobs(FEATURE_JOBS, (kind, n))
                    if kind == "SC":
                        if ph is PH["first"] and n == 7:
                            dve.wait_ge(mod_mm, 1)
                        if ph is PH["first"] and n in (3, 5):
                            dve.wait_ge(w_ready, 3 if n == 3 else 4)
                        dve.wait_ge(scores_done, T * b + n + 1)
                        V_.tensor_scalar(S[:, n, :], score[n % 2][:], 1.0, None, ALU.mult, ALU.max,
                                         accum_out=row_max[:, n:n + 1]).then_inc(scores_read, 1)
                    elif kind == "MT":
                        dve.wait_ge(scores_read, T * b + T)
                        V_.tensor_scalar(neg_max[:, 0:T], row_max[:], -1.0, None, ALU.mult).then_inc(maxT_step, 1)
                        dve.wait_ge(maxT_step, 2 * b + 1)
                        V_.scalar_tensor_tensor(neg_max[:, T:2 * T], row_max[:], -1.0, neg_max[:, 0:T].bitcast(F32),
                                                ALU.mult, ALU.subtract).then_inc(maxT_step, 1)
                        dve.wait_ge(maxT_done, b + 1)
                        V_.tensor_copy(neg_maxT, maxT_ps).then_inc(maxT_ready, 1)
                    elif kind == "SB":
                        tile = S[:, :, n * P:(n + 1) * P]
                        if n == 0:
                            dve.wait_ge(max_done, b + 1)
                        most = max_ps[:, n * P:(n + 1) * P].unsqueeze(1).broadcast_to([P, T, P])
                        V_.tensor_tensor(tile, tile, most, ALU.add).then_inc(sub_done, 1)
                    elif kind == "SM":
                        dve.wait_ge(phi_done, T * b + n + 1)
                        V_.tensor_tensor(Plo[:, n % RING, :, :], S[:, :, n * P:(n + 1) * P],
                                         Phi[:, n % RING, :, :].bitcast(F32), ALU.subtract).then_inc(plo_done, 1)
                    elif kind == "AV":
                        e, product = T * b + n + 1, av_ps[n % 2][:, 0:D]
                        dve.wait_ge(av_done, e)
                        V_.reciprocal(inv_sum[:], av_ps[n % 2][:, D:D + 1]).then_inc(inv_ready, 1)
                        dve.wait_ge(inv_ready, e)
                        if n == 0:
                            dve.wait_ge(attn_mod_in, 16 * (b + 1))
                        V_.scalar_tensor_tensor(product, product, inv_sum[:], attn_mod[:, 0, :], ALU.mult, ALU.mult).then_inc(av_scaled, 1)
                        dve.wait_ge(av_scaled, e)
                        dve.wait_ge(xc_done, T // 2 * b + n // 2 + 1)
                        V_.tensor_tensor(x_cur[:, n, :], product, x_cur[:, n, :], ALU.add).then_inc(av_read, 1)
                        dve.wait_ge(av_read, e)
                        V_.bn_stats(stats[:, n % HT, :], x_cur[:, n, :]).then_inc(x2_stats, 1)
                        wait_apart(dve, x2_stats, e)
                        V_.bn_aggr(mv2[:, n, :], stats[:, n % HT, :]).then_inc(x2_mv, 1)
                    elif kind == "MF":
                        dve.wait_ge(modT_mm, 2)
                        modulation_by_feature((2, 3), acc_modT)
                    elif kind == "GA":
                        gates()
                    elif kind == "L1":
                        e = HT * (2 * b + 2 + n)
                        wait(dve, ln1_mv, e)
                        if ph is PH["before"]:
                            dve.wait_ge(x_in[n], 16)
                        else:
                            dve.wait_ge(ln1_in, 16 * (2 * b + n + 1))
                        for t in range(HT):
                            source = x_cur[:, n * HT + t, :] if ph is PH["before"] else ln1[:, t, :]
                            V_.bn_stats(stats1[:, t, :], source).then_inc(ln1_stats, 1)
                        for t in range(HT):
                            wait_apart(dve, ln1_stats, e + t + 1)
                            V_.bn_aggr(mv1[:, n * HT + t, :], stats1[:, t, :]).then_inc(ln1_mv, 1)
                    elif kind == "SI":
                        silu()
                    elif kind == "MA":
                        dve.wait_ge(modT_mm, 1)
                        modulation_by_feature((0, 1), score[1][:, 0:4 * DK * NB])
                        dve.wait_ge(pool_const, 5)
                        V_.tensor_copy(select[:], select_sb).then_inc(w_ready, 2)
                    elif kind == "V":
                        dve.wait_ge(v_ln, HT * (2 * b + n + 1))
                        wait(dve, av_done, T * b)
                        tiles = slice(n * HT, (n + 1) * HT)
                        V_.tensor_copy(V[:, tiles, VW:VW + D], ln1[:]).then_inc(v_hi, 1)
                        dve.wait_ge(v_hi, 2 * b + n + 1)
                        V_.tensor_tensor(V[:, tiles, 0:D], ln1[:], V[:, tiles, VW:VW + D].bitcast(F32), ALU.subtract).then_inc(v_done, 1)
                    elif kind in ("TH", "T2"):
                        cols = slice(n * HR, (n + 1) * HR)
                        for kk in range(DK):
                            dve.wait_ge(feat_hi, q + kk + 1)
                            if kind == "TH":
                                V_.scalar_tensor_tensor(Llo[:, kk, cols], featT[:, kk, :], wl[:, kk:kk + 1],
                                                        Lhi[:, kk, cols].bitcast(F32), ALU.mult, ALU.subtract)
                                if ph is PH["before"]:
                                    dve.wait_ge(rhi_done, n * DK + kk + 1)
                                V_.scalar_tensor_tensor(Rlo[:, kk, cols], featT[:, kk, :], wr[:, kk:kk + 1],
                                                        Rhi[:, kk, cols].bitcast(F32), ALU.mult, ALU.subtract).then_inc(feat_done, 1)
                            else:
                                V_.tensor_tensor(h2lo[:, kk, cols], featT[:, kk, :], h2hi[:, kk, cols].bitcast(F32),
                                                 ALU.subtract).then_inc(feat_done, 1)
                    elif kind == "OUT":
                        dve.wait_ge(acc_done, NF * f + FT * (n + 1))
                        if n == 0:
                            dve.wait_ge(gb_in, 16 * b)
                            dve.wait_ge(xg_done, T // 2 * b)
                        for a in range(2):
                            V_.tensor_tensor(acc[:, a, :, :], acc[:, a, :, :], gb_all[:].unsqueeze(1).broadcast_to([P, 2, D]),
                                             ALU.mult).then_inc(acc_mul, 1)
                        for a in range(2):
                            tiles = slice(n * HT + 2 * a, n * HT + 2 * a + 2)
                            dve.wait_ge(acc_mul, 4 * f + 2 * n + a + 1)
                            V_.tensor_tensor(x_mlp[:, tiles, :], acc[:, a, :, :], x_mlp[:, tiles, :], ALU.add).then_inc(out_done, 1)

            over_batches(dve, part)

        @block.gpsimd
        def _(pool):
            G = nc.gpsimd
            G.memset(ident[:], 0.0).then_inc(pool_const, 1)
            pool.wait_ge(pool_const, 1)
            G.affine_select(out=ident[:], in_=ident[:], compare_op=ALU.not_equal, fill=1.0, base=0,
                            pattern=[[-1, P]], channel_multiplier=1).then_inc(pool_const, 1)
            G.memset(select_sb, 0.0).then_inc(pool_const, 1)
            for copy in range(2):
                pool.wait_ge(pool_const, 3 + copy)
                G.affine_select(out=select_sb, in_=select_sb, compare_op=ALU.not_equal, fill=1.0, base=-T * copy,
                                pattern=[[-1, T], [0, P]], channel_multiplier=1).then_inc(pool_const, 1)
            pool.wait_ge(const_ready, 1)

            def statistics(mv, nm, rs, h, eps_done, rstd_done, count):
                tiles = slice(h * HT, (h + 1) * HT)
                G.tensor_scalar(nm[:, tiles], mv[:, tiles, 0], -1.0, 0.0, ALU.mult, ALU.add)
                G.tensor_scalar(var_eps[:], mv[:, tiles, 1], 1.0, EPS, ALU.mult, ALU.add).then_inc(eps_done, 1)
                pool.wait_ge(eps_done, count)
                G.tensor_tensor(rs[:, tiles], var_eps[:], half_power[:], ALU.pow).then_inc(rstd_done, 1)

            def normalise(out_tiles, in_tiles, nm, rs, h, rstd_done, count, done):
                wait_apart(pool, rstd_done, count)
                for t in range(HT):
                    i = h * HT + t
                    last = G.tensor_scalar(out_tiles[:, t, :], in_tiles[:, t, :], nm[:, i:i + 1], rs[:, i:i + 1], ALU.add, ALU.mult)
                last.then_inc(done, 1)

            def part(b, ph):
                f = b - 1
                for kind, n in ph.steps["pool"]:
                    if kind == "F":
                        pool.wait_ge(hid_hi_done, NF * f + n + 1)
                        G.tensor_tensor(hid_lo[:, n % RING, :], hid[:, n % 2, :], hid_hi[:, n % RING, :].bitcast(F32),
                                        ALU.subtract).then_inc(hid_lo_done, 1)
                    elif kind == "L1":
                        wait_apart(pool, ln1_mv, HT * (2 * b + 3 + n))
                        statistics(mv1, nm1, rs1, n, ln1_eps, ln1_rstd, 2 * b + 3 + n)
                    elif kind == "L2":
                        wait_apart(pool, x2_mv, T * b + HT * (n + 1))
                        statistics(mv2, nm2, rs2, n, ln2_eps, ln2_rstd, 2 * b + n + 1)
                    elif kind == "TH":
                        pool.wait_ge(small_in, 48)
                        for kk in range(DK):
                            pool.wait_ge(col_read, n * DK + kk + 1)
                            G.tensor_scalar(Rhi[:, kk, n * HR:(n + 1) * HR], featT[:, kk, :], wr[:, kk:kk + 1], 0.0, ALU.mult, ALU.add).then_inc(rhi_done, 1)
                    elif kind == "WS":
                        for i, (lo, hi, both) in enumerate(((W1lo, W1hi, W1_sb), (W2lo, W2hi, W2_sb))):
                            pool.wait_ge(w_hi_ready, i + 1)
                            G.tensor_tensor(lo[:], both, hi[:].bitcast(F32), ALU.subtract).then_inc(w_ready, 1)
                    elif kind == "N1":
                        if ph is PH["before"]:
                            out_tiles, in_tiles = (ln1, ln2)[n], x_cur[:, n * HT:(n + 1) * HT, :]
                        else:
                            out_tiles = in_tiles = ln1
                        normalise(out_tiles, in_tiles, nm1, rs1, n, ln1_rstd, 2 * b + 3 + n, ln1_done)
                    elif kind == "N2":
                        batch = b if n == 0 else f
                        normalise(ln2, x_cur[:, n * HT:(n + 1) * HT, :], nm2, rs2, n, ln2_rstd, 2 * batch + n + 1, ln2_done)
                    elif kind == "VL":
                        pool.wait_ge(x_in[n], 16 * (b + 1))
                        if n == 0:
                            wait_apart(pool, feat_done, ph.feature_base(b))
                        else:
                            wait_apart(pool, v_done, 2 * b + 1)
                        for t in range(HT):
                            i = n * HT + t
                            G.tensor_scalar(ln1[:, t, :], x_cur[:, i, :], nm1[:, i:i + 1], rs1[:, i:i + 1], ALU.add, ALU.mult).then_inc(v_ln, 1)
                    elif kind == "XC":
                        if n == 0:
                            pool.wait_ge(attn_mod_in, 16 * (b + 1))
                        pair = x_cur[:, 2 * n:2 * n + 2, :]
                        pool.wait_ge(v_ln, HT * (2 * b + n // 2 + 1))
                        G.tensor_tensor(pair, pair, attn_mod[:, 1:2, :].broadcast_to([P, 2, D]), ALU.add).then_inc(xc_done, 1)
                    elif kind == "XG":
                        batch = b if n < 2 else f
                        if n in (0, 2):
                            wait(pool, stored[n // 2], 16 * (batch + n // 2))
                            pool.wait_ge(gb_b2_in, 16 * (batch + 1))
                        G.tensor_tensor(x_mlp[:, 2 * n:2 * n + 2, :], x_cur[:, 2 * n:2 * n + 2, :],
                                        gb_b2[:].unsqueeze(1).broadcast_to([P, 2, D]), ALU.add).then_inc(xg_done, 1)


            over_batches(pool, part)


def kernel(L0_attn_x, L0_attn_w_lhs, L0_attn_w_rhs, L0_ffn_W1, L0_ffn_b1, L0_ffn_W2, L0_ffn_b2, L0_c, L0_wmod):
    import numpy as np
    import concourse.bacc as bacc
    from concourse.bass_utils import run_bass_kernel_spmd

    def by_feature(v):
        return np.ascontiguousarray(np.asarray(v).reshape(-1, P).T)

    arrays = {
        "x": np.ascontiguousarray(L0_attn_x),
        "w_lhs": by_feature(L0_attn_w_lhs),
        "w_rhs": by_feature(L0_attn_w_rhs),
        "W1": np.ascontiguousarray(L0_ffn_W1),
        "b1": by_feature(L0_ffn_b1),
        "W2": np.ascontiguousarray(L0_ffn_W2),
        "b2": np.ascontiguousarray(L0_ffn_b2),
        "cT": np.ascontiguousarray(np.asarray(L0_c).T),
        "wmod": np.ascontiguousarray(L0_wmod),
    }
    nc = bacc.Bacc("TRN2", target_bir_lowering=False, num_devices=1)
    args = [nc.dram_tensor(name, a.shape, mybir.dt.from_np(a.dtype), kind="ExternalInput").ap() for name, a in arrays.items()]
    out = nc.dram_tensor("out", arrays["x"].shape, F32, kind="ExternalOutput").ap()
    block_kernel(nc, *args, out)
    result = run_bass_kernel_spmd(nc, [arrays], core_ids=[0])
    return result.results[0]["out"]
```

```python
from contextlib import ExitStack

import concourse.bass as bass
from concourse import mybir

F32 = mybir.dt.float32
F32R = mybir.dt.float32r
ALU = mybir.AluOpType
ACT = mybir.ActivationFunctionType

P = 128
EPS = 1e-5

STEPS = {
    "pe": """
        F.0- F.1- SC.0 SC.1 SC.2 T2.1- SC.3 SC.4 F.2- SC.5 F.3- F.4- G.0- G.1- SC.6 SC.7 G.2- F.5- G.3- MT.0
        F.6- MB.0 F.7- G.4- G.5- F.8- F.9- AV.0 G.6- G.7- TH.0+ AV.1 F.10- F.11- F.12- G.8- G.9- AV.2 G.10-
        AV.3 TH.1+ AV.4 AV.5 F.13- F.14- F.15- G.11- AV.6 G.12- T2.0 AV.7 G.13- G.14- G.15-
    """,
    "act": """
        F.0- F.1- T2.1- F.2- V.0 F.3- V.1 MT.0 F.4- F.5- F.6- EX.0 F.7- EX.1 SM.0 F.8- EX.2 SM.1 SM.2 F.9-
        L1.0+ EX.3 TH.0+ F.10- EX.4 SM.3 F.11- F.12- EX.5 EX.6 SM.4 SM.5 SM.6 EX.7 TH.1+ F.13- SM.7 F.14-
        F.15- T2.0
    """,
    "dve": """
        SC.0 SC.1 SC.2 SC.3 SC.4 XG.2- XG.3- VL.0 SC.5 T2.1- V.0 VL.1 SC.6 SC.7 V.1 MT.0 SB.0 SB.1 SB.2
        L1.0+ SM.0 SB.3 SB.4 AV.0 SM.1 OUT.0- AV.1 SM.2 TH.0+ L1.1+ SM.3 SB.5 SB.6 AV.2 SB.7 SM.4 AV.3 SM.5
        SM.6 XG.0 TH.1+ AV.4 SM.7 AV.5 AV.6 AV.7 T2.0 XG.1 OUT.1-
    """,
    "pool": """
        N2.1- F.0- F.1- F.2- F.3- XC.0 XC.1 XC.2 F.4- XC.3 F.5- F.6- L1.0+ F.7- F.8- N1.0+ F.9- F.10- F.11-
        F.12- L1.1+ N1.1+ L2.0 F.13- N2.0 F.14- F.15- L2.1
    """,
}
BEFORE_STEPS = {
    "pe": """
        TH.0+ TH.1+
    """,
    "act": """
        L1.0+ TH.0+ TH.1+
    """,
    "dve": """
        L1.0+ SI.0+ SE.0+ L1.1+ MA.0+ N1.1+ TH.0+ TH.1+
    """,
    "pool": """
        L1.0+ N1.0+ L1.1+ TH.0+ TH.1+
    """,
}
FIRST_STEPS = {
    "pe": """
        SC.0 SC.1 SC.2 MF.0 SC.3 MD.0 SC.4 SC.5 SC.6 SC.7 MT.0 MB.0 AV.0 AV.1 TH.0+ AV.2 AV.3 AV.4 TH.1+
        AV.5 T2.0 AV.6 AV.7
    """,
    "act": """
        WS.0 V.0 V.1 EX.0 SM.0 EX.1 SM.1 EX.2 EX.3 EX.4 SM.2 SM.3 L1.0+ SM.4 EX.5 EX.6 MT.0 SM.5 EX.7 TH.0+
        SM.6 TH.1+ SM.7 T2.0
    """,
    "dve": """
        SC.0 SC.1 SC.2 V.0 MF.0 SC.3 GA.0 SC.4 SC.5 SC.6 SC.7 MT.0 V.1 SB.0 SB.1 SB.2 SB.3 SB.4 L1.0+ SB.5
        AV.0 SB.6 SB.7 AV.1 AV.2 L1.1+ AV.3 TH.0+ SM.5 AV.4 TH.1+ AV.5 T2.0 AV.6 AV.7 XG.0 XG.1
    """,
    "pool": """
        VL.0 WS.0 VL.1 XC.0 XC.1 XC.2 XC.3 SM.0 SM.1 L1.0+ N1.0+ SM.2 SM.3 SM.4 L1.1+ N1.1+ L2.0 N2.0 SM.6
        SM.7 L2.1
    """,
}


class Phase:

    def __init__(self, orders, which, col_base, feature_base):
        suffixes = {"-": "prev", "+": "next"}
        self.steps = {}
        for engine, order in orders.items():
            self.steps[engine] = []
            for step in order.split():
                if suffixes.get(step[-1], "this") in which:
                    kind, number = step.rstrip("+-").split(".")
                    self.steps[engine].append((kind, int(number)))
        self.has = which
        self.col_base = col_base
        self.feature_base = feature_base

    def jobs(self, weights, until=None):
        total = 0
        for step in self.steps["pe"]:
            if step == until:
                break
            total += weights.get(step[0], 0)
        return total


COL_JOBS = {"F": 1, "T2": 2, "TH": 2}
FEATURE_JOBS = {"T2": 2, "TH": 2}


def phases(NB):
    made = {}

    def add(name, which, col_base, feature_base, steps=STEPS):
        made[name] = Phase(steps, which, col_base, feature_base)
        return made[name].jobs(COL_JOBS), made[name].jobs(FEATURE_JOBS)

    c0, f0 = add("before", {"next"}, lambda b: 0, lambda b: 0, BEFORE_STEPS)
    c1, f1 = add("first", {"this", "next"}, lambda b: c0, lambda b: f0, FIRST_STEPS)
    c1, f1 = c0 + c1, f0 + f1
    cm, fm = add("middle", {"prev", "this", "next"}, lambda b: b * cm + (c1 - cm), lambda b: b * fm + (f1 - fm))
    cl, fl = add("last", {"prev", "this"}, lambda b: c1 + (NB - 2) * cm, lambda b: f1 + (NB - 2) * fm)
    add("after", {"prev"}, lambda b: c1 + (NB - 2) * cm + cl, lambda b: f1 + (NB - 2) * fm + fl)
    return made


def block_kernel(nc, x, w_lhs, w_rhs, W1, b1, W2, b2, cT, wmod, out):
    NB, ROWS, D = x.shape
    FF = W1.shape[1]
    T = ROWS // P
    DK = D // P
    FT = FF // P
    HR = ROWS // 2
    HT = T // 2
    RING = 3
    VW = D + 2
    assert T == 8 and DK == 2 and FT == 8 and HR == 512 and NB >= 3
    NF = 2 * FT

    first_col = [P * j for j in range(T)]
    first_col[3], first_col[7] = 2 * P, 6 * P

    PH = phases(NB)
    x_rows = x.rearrange("b (h t p) d -> b h p t d", p=P, h=2)
    out_rows = out.rearrange("b (h t p) d -> b h p t d", p=P, h=2)
    mod_rows = nc.dram_tensor("mod_rows", [NB, 4, D], F32, kind="Internal").ap()

    with ExitStack() as ctx:
        sb = lambda name, shape, dt=F32: ctx.enter_context(nc.sbuf_tensor(name, shape, dt))
        psum = lambda name, shape: ctx.enter_context(nc.psum_tensor(name, shape, F32))
        sem = lambda name: ctx.enter_context(nc.semaphore(name))

        ident = sb("ident", [P, P])
        select = sb("select", [2 * T, T, P], F32R)
        W1hi, W1lo = sb("W1hi", [P, DK, FF], F32R), sb("W1lo", [P, DK, FF], F32R)
        W2hi, W2lo = sb("W2hi", [P, FT, D], F32R), sb("W2lo", [P, FT, D], F32R)
        b1T, b2T = sb("b1T", [P, FT]), sb("b2T", [P, DK])
        wl, wr = sb("wl", [P, DK]), sb("wr", [P, DK])
        mod_cols = sb("mod_cols", [P, NB, 4 * DK])
        mod_a, mod_b = sb("mod_a", [P, 2 * DK]), sb("mod_b", [P, 2 * DK])
        attn_mod, gb_b2, gb_all = sb("attn_mod", [P, 2, D]), sb("gb_b2", [P, D]), sb("gb_all", [P, D])
        S = sb("S", [P, T, ROWS])
        Phi, Plo = sb("Phi", [P, RING, T, P], F32R), sb("Plo", [P, RING, T, P], F32R)
        Lhi, Llo = sb("Lhi", [P, DK, ROWS], F32R), sb("Llo", [P, DK, ROWS], F32R)
        Rhi, Rlo = sb("Rhi", [P, DK, ROWS], F32R), sb("Rlo", [P, DK, ROWS], F32R)
        V = sb("V", [P, T, 2 * VW], F32R)
        x_cur = sb("x_cur", [P, T, D])
        x_mlp = sb("x_mlp", [P, T, D])
        ln1, ln2 = sb("ln1", [P, HT, D]), sb("ln2", [P, HT, D])
        featT = sb("featT", [P, DK, HR])
        hid = sb("hid", [P, 2, HR])
        hid_hi, hid_lo = sb("hid_hi", [P, RING, HR], F32R), sb("hid_lo", [P, RING, HR], F32R)
        h2hi, h2lo = sb("h2hi", [P, DK, ROWS], F32R), sb("h2lo", [P, DK, ROWS], F32R)
        stats, stats1 = sb("stats", [P, HT, 6]), sb("stats1", [P, HT, 6])
        mv1, nm1, rs1 = sb("mv1", [P, T, 2]), sb("nm1", [P, T]), sb("rs1", [P, T])
        mv2, nm2, rs2 = sb("mv2", [P, T, 2]), sb("nm2", [P, T]), sb("rs2", [P, T])
        var_eps, half_power = sb("var_eps", [P, HT]), sb("half_power", [P, HT])
        row_max, neg_max = sb("row_max", [P, T]), sb("neg_max", [P, 2 * T], F32R)
        neg_maxT = Phi[0:2 * T, RING - 1, 0, :]
        inv_sum = sb("inv_sum", [P, 1])

        wmod_a = S[:, 7, :].rearrange("p (k n) -> p k n", k=DK)
        wmod_b = x_mlp[:].rearrange("p (k m) d -> p k (m d)", k=DK)
        W1_sb = S[:, 3:5, :]
        W2_sb = S[:, 5:7, :].rearrange("p a (i d) -> p (a i) d", d=D)
        select_sb = S[0:2 * T, 2, :].rearrange("p (j c) -> p j c", c=P)
        cT_sb = hid[:, 0, 0:DK * NB].rearrange("p (k b) -> p k b", b=NB)
        siluT = hid[:, 0, 64:64 + DK * NB].rearrange("p (k b) -> p k b", b=NB)
        sig = hid[:, 1, 0:DK * NB].rearrange("p (k b) -> p k b", b=NB)
        sig1 = hid[:, 1, 64:64 + DK * NB].rearrange("p (k b) -> p k b", b=NB)
        sig2 = hid[:, 1, 128:128 + DK * NB].rearrange("p (k b) -> p k b", b=NB)
        signs = hid[:, 1, 256:256 + 2 * DK * NB].rearrange("p (m k b) -> p m k b", m=2, k=DK)
        mags = hid[:, 1, 320:320 + 2 * DK * NB].rearrange("p (m k b) -> p m k b", m=2, k=DK)
        row_cols = hid[:, 0, 256:256 + NB * 4 * DK]
        by_batch = hid[0:NB * 4 * DK, 0, 384:384 + P]

        score = [psum("score0", [P, ROWS]), psum("score1", [P, ROWS])]
        col = [psum("col0", [P, HR]), psum("col1", [P, HR])]
        acc = psum("acc", [P, 2, 2, D])
        mod_a_ps = score[1][:, 0:2 * DK * NB]
        mod_b_ps = acc[:, 0, 0, 0:4 * DK * NB]
        by_batch_ps = acc[0:NB * 4 * DK, 1, 0, 0:P]
        maxT_ps = score[0][0:2 * T, 0:P]
        max_ps = score[1]
        av_ps = [score[0][:, 0:VW], score[0][:, HR:HR + VW]]

        c_in, small_in = sem("c_in"), sem("small_in")
        wmod_a_in, wmod_b_in, w_in = sem("wmod_a_in"), sem("wmod_b_in"), sem("w_in")
        mods_stored = sem("mods_stored")
        ln1_in = sem("ln1_in")
        x_in = [sem("x_in0"), sem("x_in1")]
        attn_mod_in, gb_b2_in, gb_in = sem("attn_mod_in"), sem("gb_b2_in"), sem("gb_in")
        stored = [sem("stored0"), sem("stored1")]
        passed = sem("passed")
        const_ready, pool_const = sem("const_ready"), sem("pool_const")
        silu_step, sig_step = sem("silu_step"), sem("sig_step")
        modT_mm, mod_mm, mod_step = sem("modT_mm"), sem("mod_mm"), sem("mod_step")
        row_cols_ready = sem("row_cols_ready")
        modT_ready, mods_ready = sem("modT_ready"), sem("mods_ready")
        w_hi_ready, w_ready = sem("w_hi_ready"), sem("w_ready")
        scores_done, scores_read = sem("scores_done"), sem("scores_read")
        maxT_step, maxT_done, maxT_ready, max_done = sem("maxT_step"), sem("maxT_done"), sem("maxT_ready"), sem("max_done")
        sub_done, exp_done, phi_done, plo_done = sem("sub_done"), sem("exp_done"), sem("phi_done"), sem("plo_done")
        plo_pool_done, rhi_done = sem("plo_pool_done"), sem("rhi_done")
        av_done, av_read, inv_ready = sem("av_done"), sem("av_read"), sem("inv_ready")
        av_scaled, x2_stats, x2_mv = sem("av_scaled"), sem("x2_stats"), sem("x2_mv")
        xc_done, xg_done = sem("xc_done"), sem("xg_done")
        ln1_stats, ln1_mv, ln1_eps, ln1_rstd, ln1_done = sem("ln1_stats"), sem("ln1_mv"), sem("ln1_eps"), sem("ln1_rstd"), sem("ln1_done")
        ln2_eps, ln2_rstd, ln2_done = sem("ln2_eps"), sem("ln2_rstd"), sem("ln2_done")
        v_ln, v_hi, v_done = sem("v_ln"), sem("v_hi"), sem("v_done")
        col_done, col_read = sem("col_done"), sem("col_read")
        mod_a_ready, mod_b_ready = sem("mod_a_ready"), sem("mod_b_ready")
        feat_hi, feat_done = sem("feat_hi"), sem("feat_done")
        hid_hi_done, hid_lo_done = sem("hid_hi_done"), sem("hid_lo_done")
        acc_first_done, acc_done, acc_mul, out_done = sem("acc_first_done"), sem("acc_done"), sem("acc_mul"), sem("out_done")

        def wait(eng, semaphore, value):
            if not (isinstance(value, int) and value <= 0):
                eng.wait_ge(semaphore, value)

        def wait_apart(eng, semaphore, value):
            eng.wait_ge(semaphore, value)
            eng.sem_inc(passed, 1)

        def over_batches(eng, part):
            part(-1, PH["before"])
            part(0, PH["first"])
            with eng.Fori(1, NB - 1) as b:
                part(b, PH["middle"])
            part(NB - 1, PH["last"])
            part(NB, PH["after"])

        block = ctx.enter_context(nc.Block())

        @block.sync
        def _(sp):
            sp.sem_inc(stored[1], 16)
            wmod_rows = wmod.rearrange("(k p) n -> p k n", p=P)
            sp.dma_start(cT_sb, cT.rearrange("(k p) b -> p k b", p=P)).then_inc(c_in, 16)
            sp.dma_start(x_cur[:, 0:HT, :], x_rows[0, 0]).then_inc(x_in[0], 16)
            sp.dma_start(wmod_a, wmod_rows[:, :, 0:2 * D]).then_inc(wmod_a_in, 16)
            sp.dma_start(wl[:], w_lhs).then_inc(small_in, 16)
            sp.dma_start(wr[:], w_rhs).then_inc(small_in, 16)
            sp.dma_start(x_cur[:, HT:T, :], x_rows[0, 1]).then_inc(x_in[1], 16)
            sp.dma_start(wmod_b, wmod_rows[:, :, 2 * D:6 * D]).then_inc(wmod_b_in, 16)
            sp.dma_start(b1T[:], b1).then_inc(small_in, 16)
            sp.dma_start(b2T[:], b2).then_inc(small_in, 16)
            sp.dma_start(W1_sb, W1.rearrange("(k p) n -> p k n", p=P)).then_inc(w_in, 16)
            sp.dma_start(W2_sb, W2.rearrange("(i p) d -> p i d", p=P)).then_inc(w_in, 16)
            sp.wait_ge(mods_ready, 1)
            sp.dma_start(mod_rows.rearrange("b a (k c) -> (b a k) c", c=P), by_batch).then_inc(mods_stored, 16)
            sp.wait_ge(mods_stored, 16)

            def part(b, ph):
                f = b - 1
                if "this" in ph.has:
                    wait(sp, av_read, T * b)
                    sp.dma_start(attn_mod[:].rearrange("p a d -> p (a d)"),
                                 mod_rows[b, 0:2, :].rearrange("a d -> (a d)").partition_broadcast(P)).then_inc(attn_mod_in, 16)
                if "prev" in ph.has:
                    sp.dma_start(gb_all[:], mod_rows[f, 2, :].partition_broadcast(P)).then_inc(gb_in, 16)
                if "this" in ph.has:
                    if ph is not PH["first"]:
                        sp.wait_ge(xg_done, T // 2 * b)
                        sp.dma_start(x_cur[:, HT:T, :], x_rows[b, 1]).then_inc(x_in[1], 16)
                    sp.dma_start(gb_b2[:], mod_rows[b, 3, :].partition_broadcast(P)).then_inc(gb_b2_in, 16)
                if "next" in ph.has:
                    sp.wait_ge(v_done, 2 * b + 2)
                    sp.dma_start(ln1[:], x_rows[b + 1, 0]).then_inc(ln1_in, 16)
                if "prev" in ph.has:
                    sp.wait_ge(out_done, 4 * f + 2)
                    sp.dma_start(out_rows[f, 0], x_mlp[:, 0:HT, :]).then_inc(stored[0], 16)
                if "next" in ph.has:
                    sp.wait_ge(col_done, ph.col_base(b) + ph.jobs(COL_JOBS, ("TH", 0)) + DK)
                    sp.dma_start(ln1[:], x_rows[b + 1, 1]).then_inc(ln1_in, 16)
                    sp.wait_ge(xg_done, T // 2 * b + 2)
                    sp.dma_start(x_cur[:, 0:HT, :], x_rows[b + 1, 0]).then_inc(x_in[0], 16)
                if "prev" in ph.has:
                    for a in range(2):
                        sp.wait_ge(out_done, 4 * f + 3 + a)
                        sp.dma_start(out_rows[f, 1][:, 2 * a:2 * a + 2, :],
                                     x_mlp[:, HT + 2 * a:HT + 2 * a + 2, :]).then_inc(stored[1], 16)

            part(0, PH["first"])
            with sp.Fori(1, NB - 1) as b:
                part(b, PH["middle"])
            part(NB - 1, PH["last"])
            part(NB, PH["after"])
            sp.wait_ge(stored[0], 16 * NB)
            sp.wait_ge(stored[1], 32 * NB + 16)

        @block.tensor
        def _(pe):
            def wmod_part(kk, m, start, width):
                staged, at = (wmod_a, m * D) if m < 2 else (wmod_b, (m - 2) * D)
                return staged[:, kk, at + start:at + start + width]

            def modulation_by_feature(parts, modT):
                for n, m in enumerate(parts):
                    for k in range(DK):
                        for kk in range(DK):
                            last = nc.tensor.matmul(modT[:, (n * DK + k) * NB:(n * DK + k + 1) * NB],
                                                    wmod_part(kk, m, k * P, P), siluT[:, kk, :],
                                                    start=(kk == 0), stop=(kk == DK - 1))
                last.then_inc(modT_mm, 1)

            pe.wait_ge(silu_step, 1)
            pe.wait_ge(wmod_a_in, 16)
            modulation_by_feature((1, 0), mod_a_ps)

            pool_lo = [n for kind, n in PH["first"].steps["pool"] if kind == "SM"]
            dve_lo = [n for n in range(T) if n not in pool_lo]

            def wait_lo(ph, b, n):
                if ph is not PH["first"]:
                    pe.wait_ge(plo_done, T * (b - 1) + len(dve_lo) + n + 1)
                elif n in pool_lo:
                    pe.wait_ge(plo_pool_done, pool_lo.index(n) + 1)
                else:
                    pe.wait_ge(plo_done, dve_lo.index(n) + 1)

            def part(b, ph):
                f = b - 1
                column, features = ph.col_base(b), ph.feature_base(b)

                def second_layer(i):
                    slot, it = i % RING, i % FT
                    pe.wait_ge(hid_hi_done, NF * f + i + 1)
                    if i == 0:
                        pe.wait_ge(xg_done, T // 2 * f + T // 2)
                    elif it == 0:
                        pe.wait_ge(out_done, 4 * f + 2)
                    for tiles in [range(HT)] if it < FT - 1 else [range(0, 2), range(2, HT)]:
                        for t in tiles:
                            o, hi = acc[:, t // 2, t % 2, :], hid_hi[:, slot, t * P:(t + 1) * P]
                            nc.tensor.matmul(o, hi, W2hi[:, it, :], start=(it == 0 and t % 2 == 0), stop=False, skip_group_check=True)
                            nc.tensor.matmul(o, hi, W2lo[:, it, :], start=False, stop=False, skip_group_check=True)
                        if tiles[0] == 0:
                            pe.wait_ge(hid_lo_done, NF * f + i + 1)
                        for t in tiles:
                            o, lo = acc[:, t // 2, t % 2, :], hid_lo[:, slot, t * P:(t + 1) * P]
                            last = nc.tensor.matmul(o, lo, W2hi[:, it, :], start=False, stop=(it == FT - 1), skip_group_check=True)
                        if tiles[-1] == 1:
                            last.then_inc(acc_first_done, 1)
                    last.then_inc(acc_done, 1)

                for kind, n in ph.steps["pe"]:
                    c = column + ph.jobs(COL_JOBS, (kind, n))
                    cb = ph.jobs(COL_JOBS, (kind, n)) % 2
                    if kind == "SC":
                        if n == 0:
                            pe.wait_ge(feat_done, features - DK if ph is PH["first"] else features)
                            wait(pe, av_read, T * b)
                        elif ph is PH["first"] and n == 1:
                            pe.wait_ge(modT_ready, 2)
                        elif n == 1:
                            pe.wait_ge(sub_done, T * b)
                        else:
                            pe.wait_ge(scores_read, T * b + n - 1)
                        at = first_col[n]
                        for lo_col in range(0, ROWS, HR):
                            start_col = max(at, lo_col)
                            width = lo_col + HR - start_col
                            if width <= 0:
                                continue
                            if ph is PH["first"] and n == 0 and lo_col > 0:
                                pe.wait_ge(feat_done, features)
                            o = score[n % 2][:, start_col:lo_col + HR]
                            tile, cols = slice(n * P, (n + 1) * P), slice(start_col, lo_col + HR)
                            for kk in range(DK):
                                nc.tensor.matmul(o, Lhi[:, kk, tile], Rhi[:, kk, cols], start=(kk == 0), stop=False)
                                nc.tensor.matmul(o, Lhi[:, kk, tile], Rlo[:, kk, cols], start=False, stop=False)
                                last = nc.tensor.matmul(o, Llo[:, kk, tile], Rhi[:, kk, cols], start=False, stop=(kk == DK - 1))
                        for i in range(at // P):
                            if i == at // P - 1:
                                pe.wait_ge(scores_read, T * b + i + 1)
                            last = nc.tensor.transpose(score[n % 2][:, i * P:(i + 1) * P], S[:, i, n * P:(n + 1) * P], ident[:])
                        last.then_inc(scores_done, 1)
                    elif kind == "F":
                        half, it = n // FT, n % FT
                        if it == 0:
                            pe.wait_ge(feat_done, features + DK * half)
                        pe.wait_ge(col_read, c - 1)
                        tile, cols = slice(it * P, (it + 1) * P), slice(half * HR, (half + 1) * HR)
                        for kk in range(DK):
                            nc.tensor.matmul(col[cb][:], W1hi[:, kk, tile], h2hi[:, kk, cols], start=(kk == 0), stop=False)
                            nc.tensor.matmul(col[cb][:], W1hi[:, kk, tile], h2lo[:, kk, cols], start=False, stop=False)
                            last = nc.tensor.matmul(col[cb][:], W1lo[:, kk, tile], h2hi[:, kk, cols], start=False, stop=(kk == DK - 1))
                        last.then_inc(col_done, 1)
                    elif kind == "G":
                        second_layer(n)
                    elif kind == "MF":
                        pe.wait_ge(wmod_b_in, 16)
                        modulation_by_feature((4, 3, 2, 5), mod_b_ps)
                    elif kind == "MD":
                        pe.wait_ge(row_cols_ready, 1)
                        nc.tensor.transpose(by_batch_ps, row_cols, ident[:]).then_inc(mod_mm, 1)
                    elif kind in ("TH", "T2"):
                        if kind == "TH":
                            pe.wait_ge(ln1_done, 2 * (b + 1) + n + 1)
                            ln = ln2 if ph is PH["before"] and n == 1 else ln1
                            if ph is PH["before"] and n == 0:
                                pe.wait_ge(pool_const, 2)
                        else:
                            pe.wait_ge(ln2_done, 2 * (b if n == 0 else f) + n + 1)
                            ln = ln2
                        for kk in range(DK):
                            wait(pe, col_read, c + kk - 1)
                            for t in range(HT):
                                last = nc.tensor.transpose(col[(cb + kk) % 2][:, t * P:(t + 1) * P], ln[:, t, kk * P:(kk + 1) * P], ident[:])
                            last.then_inc(col_done, 1)
                    elif kind == "MT":
                        if ph is PH["first"]:
                            pe.wait_ge(w_ready, 4)
                        pe.wait_ge(maxT_step, 2 * b + 2)
                        nc.tensor.transpose(maxT_ps, neg_max[:].bitcast(F32), ident[:]).then_inc(maxT_done, 1)
                    elif kind == "MB":
                        pe.wait_ge(maxT_ready, b + 1)
                        for j in range(T):
                            last = nc.tensor.matmul(max_ps[:, j * P:(j + 1) * P], select[:, j, :], neg_maxT, start=True, stop=True)
                        last.then_inc(max_done, 1)
                    elif kind == "AV":
                        pe.wait_ge(phi_done, T * b + n + 1)
                        if n == 0:
                            pe.wait_ge(v_done, 2 * b + 2)
                        if n >= 2:
                            pe.wait_ge(av_read, T * b + n - 1)
                        slot, o = n % RING, av_ps[n % 2]
                        for t in range(T):
                            nc.tensor.matmul(o, Phi[:, slot, t, :], V[:, t, 0:VW], start=(t == 0), stop=False)
                            nc.tensor.matmul(o[:, 0:D], Phi[:, slot, t, :], V[:, t, VW:VW + D], start=False, stop=False)
                        wait_lo(ph, b, n)
                        for t in range(T):
                            last = nc.tensor.matmul(o, Plo[:, slot, t, :], V[:, t, VW:2 * VW], start=False, stop=(t == T - 1))
                        last.then_inc(av_done, 1)

            over_batches(pe, part)

        @block.scalar
        def _(act):
            act.wait_ge(c_in, 16)
            nc.scalar.activation(sig, cT_sb, ACT.Exp, scale=-1.0).then_inc(sig_step, 1)

            def part(b, ph):
                f = b - 1
                column, features = ph.col_base(b), ph.feature_base(b)
                for kind, n in ph.steps["act"]:
                    c = column + ph.jobs(COL_JOBS, (kind, n))
                    cb = ph.jobs(COL_JOBS, (kind, n)) % 2
                    q = features + ph.jobs(FEATURE_JOBS, (kind, n))
                    if kind == "F":
                        act.wait_ge(col_done, c + 1)
                        if n >= 2:
                            act.wait_ge(hid_lo_done, NF * f + n - 1)
                        nc.scalar.activation(hid[:, n % 2, :], col[cb][:], ACT.Relu, bias=b1T[:, n % FT:n % FT + 1]).then_inc(col_read, 1)
                        act.wait_ge(col_read, c + 1)
                        if n >= RING:
                            act.wait_ge(acc_done, NF * f + n - RING + 1)
                        nc.scalar.activation(hid_hi[:, n % RING, :], hid[:, n % 2, :], ACT.Copy).then_inc(hid_hi_done, 1)
                    elif kind in ("TH", "T2"):
                        half = n
                        mod = mod_a if kind == "TH" else mod_b
                        if kind == "TH":
                            act.wait_ge(mod_a_ready, b + 2)
                        else:
                            act.wait_ge(mod_b_ready, (b if n == 0 else f) + 1)
                        cols = slice(half * HR, (half + 1) * HR)
                        for kk in range(DK):
                            act.wait_ge(col_done, c + kk + 1)
                            wait(act, feat_done, q + kk - 1)
                            nc.scalar.activation(featT[:, kk, :], col[(cb + kk) % 2][:], ACT.Identity,
                                                 scale=mod[:, kk:kk + 1], bias=mod[:, DK + kk:DK + kk + 1]).then_inc(col_read, 1)
                            act.wait_ge(col_read, c + kk + 1)
                            if kind == "TH":
                                last = nc.scalar.activation(Lhi[:, kk, cols], featT[:, kk, :], ACT.Copy, scale=wl[:, kk:kk + 1])
                                if ph is not PH["before"]:
                                    last = nc.scalar.activation(Rhi[:, kk, cols], featT[:, kk, :], ACT.Copy, scale=wr[:, kk:kk + 1])
                                last.then_inc(feat_hi, 1)
                            else:
                                nc.scalar.activation(h2hi[:, kk, cols], featT[:, kk, :], ACT.Copy).then_inc(feat_hi, 1)
                    elif kind == "WS":
                        act.wait_ge(w_in, 32)
                        nc.scalar.activation(W1hi[:], W1_sb, ACT.Copy).then_inc(w_hi_ready, 1)
                        nc.scalar.activation(W2hi[:], W2_sb, ACT.Copy).then_inc(w_hi_ready, 1)
                    elif kind == "L1" and n == 0:
                        if ph is PH["before"]:
                            act.wait_ge(modT_ready, 2)
                            act.wait_ge(small_in, 64)
                        nc.scalar.activation(mod_a[:], mod_cols[:, b + 1, 0:2 * DK], ACT.Copy).then_inc(mod_a_ready, 1)
                    elif kind == "MT":
                        if ph is PH["first"]:
                            act.wait_ge(modT_ready, 4)
                        nc.scalar.activation(mod_b[:], mod_cols[:, b, 2 * DK:4 * DK], ACT.Copy).then_inc(mod_b_ready, 1)
                    elif kind == "V":
                        act.wait_ge(v_ln, HT * (2 * b + n + 1))
                        wait(act, av_done, T * b)
                        nc.scalar.activation(V[:, n * HT:(n + 1) * HT, VW:VW + D], ln1[:], ACT.Copy).then_inc(v_hi, 1)
                    elif kind == "EX":
                        tile = S[:, :, n * P:(n + 1) * P]
                        act.wait_ge(sub_done, T * b + n + 1)
                        nc.scalar.activation(tile, tile, ACT.Exp).then_inc(exp_done, 1)
                    elif kind == "SM":
                        act.wait_ge(exp_done, T * b + n + 1)
                        wait(act, av_done, T * b + max(n - RING + 1, 0))
                        nc.scalar.activation(Phi[:, n % RING, :, :], S[:, :, n * P:(n + 1) * P], ACT.Copy).then_inc(phi_done, 1)

            over_batches(act, part)

        @block.vector
        def _(dve):
            V_ = nc.vector
            V_.memset(half_power[:], -0.5).then_inc(const_ready, 1)
            V_.memset(V[:, :, D:D + 1].bitcast(F32), 1.0)
            V_.memset(V[:, :, D + 1:VW].bitcast(F32), 0.0)
            V_.memset(V[:, :, VW + D:VW + D + 1].bitcast(F32), 1.0)
            V_.memset(V[:, :, VW + D + 1:2 * VW].bitcast(F32), 0.0)

            def silu():
                dve.wait_ge(sig_step, 1)
                V_.tensor_scalar(sig1, sig, 1.0, None, ALU.add).then_inc(sig_step, 1)
                dve.wait_ge(sig_step, 2)
                V_.reciprocal(sig2, sig1).then_inc(sig_step, 1)
                dve.wait_ge(sig_step, 3)
                V_.tensor_tensor(siluT, cT_sb, sig2, ALU.mult).then_inc(silu_step, 1)

            def modulation_by_feature(first, modT):
                modT = modT.rearrange("p (n b) -> p b n", b=NB)
                for n in range(2):
                    V_.tensor_scalar(mod_cols[:, :, (first + n) * DK:(first + n + 1) * DK], modT[:, :, n * DK:(n + 1) * DK],
                                     1.0 - n, None, ALU.add).then_inc(modT_ready, 1)

            def gates():
                g = mod_b_ps[:, 2 * DK * NB:4 * DK * NB].rearrange("p (m k b) -> p m k b", m=2, k=DK)
                V_.tensor_scalar(signs, g, 0.0, 2.0, ALU.is_ge, ALU.mult).then_inc(mod_step, 1)
                V_.tensor_scalar(mags, g, -1.0, None, ALU.mult).then_inc(mod_step, 1)
                dve.wait_ge(mod_step, 2)
                V_.tensor_tensor(mags, mags, g, ALU.max).then_inc(mod_step, 1)
                dve.wait_ge(mod_step, 3)
                V_.tensor_scalar(mags, mags, 0.25, None, ALU.max).then_inc(mod_step, 1)
                dve.wait_ge(mod_step, 4)
                out = row_cols.rearrange("p (b a k) -> p a k b", b=NB, a=4)
                ga, gb = mags[:, 0, :, :], out[:, 2, :, :]
                V_.scalar_tensor_tensor(ga, signs[:, 0, :, :], -1.0, ga, ALU.add, ALU.mult).then_inc(mod_step, 1)
                V_.scalar_tensor_tensor(gb, signs[:, 1, :, :], -1.0, mags[:, 1, :, :], ALU.add, ALU.mult).then_inc(mod_step, 1)
                dve.wait_ge(mod_step, 6)
                mod = mod_cols[:].rearrange("p b (n k) -> p n k b", k=DK)
                V_.tensor_tensor(out[:, 0, :, :], mod[:, 0, :, :], ga, ALU.mult)
                V_.tensor_tensor(out[:, 1, :, :], mod[:, 1, :, :], ga, ALU.mult)
                V_.tensor_tensor(out[:, 3, :, :], gb, b2T[:].unsqueeze(2).broadcast_to([P, DK, NB]), ALU.mult).then_inc(row_cols_ready, 1)

            def normalise(out_tiles, in_tiles, nm, rs, h, rstd_done, count, done):
                wait_apart(dve, rstd_done, count)
                for t in range(HT):
                    i = h * HT + t
                    last = V_.tensor_scalar(out_tiles[:, t, :], in_tiles[:, t, :], nm[:, i:i + 1], rs[:, i:i + 1], ALU.add, ALU.mult)
                last.then_inc(done, 1)

            def part(b, ph):
                f = b - 1
                features = ph.feature_base(b)
                for kind, n in ph.steps["dve"]:
                    q = features + ph.jobs(FEATURE_JOBS, (kind, n))
                    if kind == "SC":
                        if ph is PH["first"] and n == 7:
                            dve.wait_ge(modT_mm, 1)
                        if ph is PH["first"] and n in (3, 5):
                            dve.wait_ge(w_ready, 3 if n == 3 else 4)
                        dve.wait_ge(scores_done, T * b + n + 1)
                        V_.tensor_scalar(S[:, n, :], score[n % 2][:], 1.0, None, ALU.mult, ALU.max,
                                         accum_out=row_max[:, n:n + 1]).then_inc(scores_read, 1)
                    elif kind == "MT":
                        dve.wait_ge(scores_read, T * b + T)
                        V_.tensor_scalar(neg_max[:, 0:T], row_max[:], -1.0, None, ALU.mult).then_inc(maxT_step, 1)
                        dve.wait_ge(maxT_step, 2 * b + 1)
                        V_.scalar_tensor_tensor(neg_max[:, T:2 * T], row_max[:], -1.0, neg_max[:, 0:T].bitcast(F32),
                                                ALU.mult, ALU.subtract).then_inc(maxT_step, 1)
                        dve.wait_ge(maxT_done, b + 1)
                        V_.tensor_copy(neg_maxT, maxT_ps).then_inc(maxT_ready, 1)
                    elif kind == "SB":
                        tile = S[:, :, n * P:(n + 1) * P]
                        if n == 0:
                            dve.wait_ge(max_done, b + 1)
                        most = max_ps[:, n * P:(n + 1) * P].unsqueeze(1).broadcast_to([P, T, P])
                        V_.tensor_tensor(tile, tile, most, ALU.add).then_inc(sub_done, 1)
                    elif kind == "SM":
                        dve.wait_ge(phi_done, T * b + n + 1)
                        V_.tensor_tensor(Plo[:, n % RING, :, :], S[:, :, n * P:(n + 1) * P],
                                         Phi[:, n % RING, :, :].bitcast(F32), ALU.subtract).then_inc(plo_done, 1)
                    elif kind == "AV":
                        e, product = T * b + n + 1, av_ps[n % 2][:, 0:D]
                        dve.wait_ge(av_done, e)
                        V_.reciprocal(inv_sum[:], av_ps[n % 2][:, D:D + 1]).then_inc(inv_ready, 1)
                        dve.wait_ge(inv_ready, e)
                        if n == 0:
                            dve.wait_ge(attn_mod_in, 16 * (b + 1))
                        V_.scalar_tensor_tensor(product, product, inv_sum[:], attn_mod[:, 0, :], ALU.mult, ALU.mult).then_inc(av_scaled, 1)
                        dve.wait_ge(av_scaled, e)
                        dve.wait_ge(xc_done, T // 2 * b + n // 2 + 1)
                        V_.tensor_tensor(x_cur[:, n, :], product, x_cur[:, n, :], ALU.add).then_inc(av_read, 1)
                        dve.wait_ge(av_read, e)
                        V_.bn_stats(stats[:, n % HT, :], x_cur[:, n, :]).then_inc(x2_stats, 1)
                        wait_apart(dve, x2_stats, e)
                        V_.bn_aggr(mv2[:, n, :], stats[:, n % HT, :]).then_inc(x2_mv, 1)
                    elif kind == "MF":
                        dve.wait_ge(modT_mm, 2)
                        modulation_by_feature(2, mod_b_ps)
                        gates()
                    elif kind == "GA":
                        dve.wait_ge(mod_mm, 1)
                        V_.tensor_copy(by_batch, by_batch_ps).then_inc(mods_ready, 1)
                    elif kind == "L1":
                        e = HT * (2 * b + 2 + n)
                        wait(dve, ln1_mv, e)
                        if ph is PH["before"]:
                            dve.wait_ge(x_in[n], 16)
                        else:
                            dve.wait_ge(ln1_in, 16 * (2 * b + n + 1))
                        for t in range(HT):
                            source = x_cur[:, n * HT + t, :] if ph is PH["before"] else ln1[:, t, :]
                            V_.bn_stats(stats1[:, t, :], source).then_inc(ln1_stats, 1)
                        for t in range(HT):
                            wait_apart(dve, ln1_stats, e + t + 1)
                            V_.bn_aggr(mv1[:, n * HT + t, :], stats1[:, t, :]).then_inc(ln1_mv, 1)
                    elif kind == "SI":
                        silu()
                    elif kind == "MA":
                        dve.wait_ge(modT_mm, 1)
                        modulation_by_feature(0, mod_a_ps)
                    elif kind == "SE":
                        dve.wait_ge(pool_const, 5)
                        V_.tensor_copy(select[:], select_sb).then_inc(w_ready, 2)
                    elif kind == "V":
                        tiles = slice(n * HT, (n + 1) * HT)
                        dve.wait_ge(v_hi, 2 * b + n + 1)
                        V_.tensor_tensor(V[:, tiles, 0:D], ln1[:], V[:, tiles, VW:VW + D].bitcast(F32), ALU.subtract).then_inc(v_done, 1)
                    elif kind in ("TH", "T2"):
                        cols = slice(n * HR, (n + 1) * HR)
                        for kk in range(DK):
                            dve.wait_ge(feat_hi, q + kk + 1)
                            if kind == "TH":
                                V_.scalar_tensor_tensor(Llo[:, kk, cols], featT[:, kk, :], wl[:, kk:kk + 1],
                                                        Lhi[:, kk, cols].bitcast(F32), ALU.mult, ALU.subtract)
                                if ph is PH["before"]:
                                    dve.wait_ge(rhi_done, n * DK + kk + 1)
                                V_.scalar_tensor_tensor(Rlo[:, kk, cols], featT[:, kk, :], wr[:, kk:kk + 1],
                                                        Rhi[:, kk, cols].bitcast(F32), ALU.mult, ALU.subtract).then_inc(feat_done, 1)
                            else:
                                V_.tensor_tensor(h2lo[:, kk, cols], featT[:, kk, :], h2hi[:, kk, cols].bitcast(F32),
                                                 ALU.subtract).then_inc(feat_done, 1)
                    elif kind == "OUT":
                        if n == 0:
                            dve.wait_ge(gb_in, 16 * b)
                            dve.wait_ge(xg_done, T // 2 * b)
                        for a in range(2):
                            if a == 0:
                                dve.wait_ge(acc_first_done, 2 * f + n + 1)
                            else:
                                dve.wait_ge(acc_done, NF * f + FT * (n + 1))
                            V_.tensor_tensor(acc[:, a, :, :], acc[:, a, :, :], gb_all[:].unsqueeze(1).broadcast_to([P, 2, D]),
                                             ALU.mult).then_inc(acc_mul, 1)
                            tiles = slice(n * HT + 2 * a, n * HT + 2 * a + 2)
                            dve.wait_ge(acc_mul, 4 * f + 2 * n + a + 1)
                            V_.tensor_tensor(x_mlp[:, tiles, :], acc[:, a, :, :], x_mlp[:, tiles, :], ALU.add).then_inc(out_done, 1)
                    elif kind == "N1":
                        if ph is PH["before"]:
                            if n == 1:
                                dve.wait_ge(ln1_done, 1)
                            out_tiles, in_tiles = (ln1, ln2)[n], x_cur[:, n * HT:(n + 1) * HT, :]
                        else:
                            out_tiles = in_tiles = ln1
                        normalise(out_tiles, in_tiles, nm1, rs1, n, ln1_rstd, 2 * b + 3 + n, ln1_done)
                    elif kind == "VL":
                        dve.wait_ge(x_in[n], 16 * (b + 1))
                        if n == 0:
                            wait_apart(dve, feat_done, ph.feature_base(b))
                        else:
                            wait_apart(dve, v_done, 2 * b + 1)
                        for t in range(HT):
                            i = n * HT + t
                            V_.tensor_scalar(ln1[:, t, :], x_cur[:, i, :], nm1[:, i:i + 1], rs1[:, i:i + 1], ALU.add, ALU.mult).then_inc(v_ln, 1)
                    elif kind == "XG":
                        batch = b if n < 2 else f
                        if n in (0, 2):
                            wait(dve, stored[n // 2], 16 * batch if n == 0 else 32 * batch + 16)
                            dve.wait_ge(gb_b2_in, 16 * (batch + 1))
                        V_.tensor_tensor(x_mlp[:, 2 * n:2 * n + 2, :], x_cur[:, 2 * n:2 * n + 2, :],
                                        gb_b2[:].unsqueeze(1).broadcast_to([P, 2, D]), ALU.add).then_inc(xg_done, 1)

            over_batches(dve, part)

        @block.gpsimd
        def _(pool):
            G = nc.gpsimd
            G.memset(ident[:], 0.0).then_inc(pool_const, 1)
            pool.wait_ge(pool_const, 1)
            G.affine_select(out=ident[:], in_=ident[:], compare_op=ALU.not_equal, fill=1.0, base=0,
                            pattern=[[-1, P]], channel_multiplier=1).then_inc(pool_const, 1)
            G.memset(select_sb, 0.0).then_inc(pool_const, 1)
            for copy in range(2):
                pool.wait_ge(pool_const, 3 + copy)
                G.affine_select(out=select_sb, in_=select_sb, compare_op=ALU.not_equal, fill=1.0, base=-T * copy,
                                pattern=[[-1, T], [0, P]], channel_multiplier=1).then_inc(pool_const, 1)
            pool.wait_ge(const_ready, 1)

            def statistics(mv, nm, rs, h, eps_done, rstd_done, count):
                tiles = slice(h * HT, (h + 1) * HT)
                G.tensor_scalar(nm[:, tiles], mv[:, tiles, 0], -1.0, 0.0, ALU.mult, ALU.add)
                G.tensor_scalar(var_eps[:], mv[:, tiles, 1], 1.0, EPS, ALU.mult, ALU.add).then_inc(eps_done, 1)
                pool.wait_ge(eps_done, count)
                G.tensor_tensor(rs[:, tiles], var_eps[:], half_power[:], ALU.pow).then_inc(rstd_done, 1)

            def normalise(out_tiles, in_tiles, nm, rs, h, rstd_done, count, done):
                wait_apart(pool, rstd_done, count)
                for t in range(HT):
                    i = h * HT + t
                    last = G.tensor_scalar(out_tiles[:, t, :], in_tiles[:, t, :], nm[:, i:i + 1], rs[:, i:i + 1], ALU.add, ALU.mult)
                last.then_inc(done, 1)

            def part(b, ph):
                f = b - 1
                for kind, n in ph.steps["pool"]:
                    if kind == "F":
                        pool.wait_ge(hid_hi_done, NF * f + n + 1)
                        G.tensor_tensor(hid_lo[:, n % RING, :], hid[:, n % 2, :], hid_hi[:, n % RING, :].bitcast(F32),
                                        ALU.subtract).then_inc(hid_lo_done, 1)
                    elif kind == "L1":
                        wait_apart(pool, ln1_mv, HT * (2 * b + 3 + n))
                        statistics(mv1, nm1, rs1, n, ln1_eps, ln1_rstd, 2 * b + 3 + n)
                    elif kind == "L2":
                        wait_apart(pool, x2_mv, T * b + HT * (n + 1))
                        statistics(mv2, nm2, rs2, n, ln2_eps, ln2_rstd, 2 * b + n + 1)
                    elif kind == "TH":
                        pool.wait_ge(small_in, 64)
                        for kk in range(DK):
                            pool.wait_ge(col_read, n * DK + kk + 1)
                            G.tensor_scalar(Rhi[:, kk, n * HR:(n + 1) * HR], featT[:, kk, :], wr[:, kk:kk + 1], 0.0, ALU.mult, ALU.add).then_inc(rhi_done, 1)
                    elif kind == "WS":
                        for i, (lo, hi, both) in enumerate(((W1lo, W1hi, W1_sb), (W2lo, W2hi, W2_sb))):
                            pool.wait_ge(w_hi_ready, i + 1)
                            G.tensor_tensor(lo[:], both, hi[:].bitcast(F32), ALU.subtract).then_inc(w_ready, 1)
                    elif kind == "N1":
                        if ph is PH["before"]:
                            if n == 1:
                                pool.wait_ge(ln1_done, 1)
                            out_tiles, in_tiles = (ln1, ln2)[n], x_cur[:, n * HT:(n + 1) * HT, :]
                        else:
                            out_tiles = in_tiles = ln1
                        normalise(out_tiles, in_tiles, nm1, rs1, n, ln1_rstd, 2 * b + 3 + n, ln1_done)
                    elif kind == "N2":
                        batch = b if n == 0 else f
                        normalise(ln2, x_cur[:, n * HT:(n + 1) * HT, :], nm2, rs2, n, ln2_rstd, 2 * batch + n + 1, ln2_done)
                    elif kind == "VL":
                        pool.wait_ge(x_in[n], 16 * (b + 1))
                        if n == 0:
                            wait_apart(pool, feat_done, ph.feature_base(b))
                        else:
                            wait_apart(pool, v_done, 2 * b + 1)
                        for t in range(HT):
                            i = n * HT + t
                            G.tensor_scalar(ln1[:, t, :], x_cur[:, i, :], nm1[:, i:i + 1], rs1[:, i:i + 1], ALU.add, ALU.mult).then_inc(v_ln, 1)
                    elif kind == "XC":
                        if n == 0:
                            pool.wait_ge(attn_mod_in, 16 * (b + 1))
                        pair = x_cur[:, 2 * n:2 * n + 2, :]
                        pool.wait_ge(v_ln, HT * (2 * b + n // 2 + 1))
                        G.tensor_tensor(pair, pair, attn_mod[:, 1:2, :].broadcast_to([P, 2, D]), ALU.add).then_inc(xc_done, 1)
                    elif kind == "SM":
                        pool.wait_ge(phi_done, T * b + n + 1)
                        G.tensor_tensor(Plo[:, n % RING, :, :], S[:, :, n * P:(n + 1) * P],
                                        Phi[:, n % RING, :, :].bitcast(F32), ALU.subtract).then_inc(plo_pool_done, 1)

            over_batches(pool, part)


def kernel(L0_attn_x, L0_attn_w_lhs, L0_attn_w_rhs, L0_ffn_W1, L0_ffn_b1, L0_ffn_W2, L0_ffn_b2, L0_c, L0_wmod):
    import numpy as np
    import concourse.bacc as bacc
    from concourse.bass_utils import run_bass_kernel_spmd

    def by_feature(v):
        return np.ascontiguousarray(np.asarray(v).reshape(-1, P).T)

    arrays = {
        "x": np.ascontiguousarray(L0_attn_x),
        "w_lhs": by_feature(L0_attn_w_lhs),
        "w_rhs": by_feature(L0_attn_w_rhs),
        "W1": np.ascontiguousarray(L0_ffn_W1),
        "b1": by_feature(L0_ffn_b1),
        "W2": np.ascontiguousarray(L0_ffn_W2),
        "b2": by_feature(L0_ffn_b2),
        "cT": np.ascontiguousarray(np.asarray(L0_c).T),
        "wmod": np.ascontiguousarray(L0_wmod),
    }
    nc = bacc.Bacc("TRN2", target_bir_lowering=False, num_devices=1)
    args = [nc.dram_tensor(name, a.shape, mybir.dt.from_np(a.dtype), kind="ExternalInput").ap() for name, a in arrays.items()]
    out = nc.dram_tensor("out", arrays["x"].shape, F32, kind="ExternalOutput").ap()
    block_kernel(nc, *args, out)
    result = run_bass_kernel_spmd(nc, [arrays], core_ids=[0])
    return result.results[0]["out"]
```
